# Optimizing a Trainium2 kernel written in Bass

```python
import numpy as np
import jax
import jax.numpy as jnp

def _softmax(x, axis=-1):
    return jax.nn.softmax(x, axis=axis)

def _gelu(x):
    return jax.nn.gelu(x, approximate=True)

def _silu(x):
    return jax.nn.silu(x)

def _sigmoid(x):
    return jax.nn.sigmoid(x)

def _layernorm(x, axis=-1, eps=1e-05):
    m = jnp.mean(x, axis=axis, keepdims=True)
    v = jnp.var(x, axis=axis, keepdims=True)
    return (x - m) / jnp.sqrt(v + eps)

def _scatter_add(tgt, idx, src, axis=0):
    return tgt.at[idx].add(src)

def _segment_sum(src, seg, n):
    return jax.ops.segment_sum(src, seg, n)
kernel_name = 'mk_decoder_postln_d1_seqx_r8_bfdc5b'

def setup_inputs(seed: int=0):
    np.random.seed(seed)
    _w = jnp.asarray

    def _rec_inputs():
        import jax
        import jax.numpy as jnp
        _rk = jax.random.key(seed)
        x = -0.0002928 + 1 * jax.random.normal(jax.random.fold_in(_rk, 1), (32, 128, 128), jnp.float32)
        _lenS = 128 - jax.random.randint(jax.random.fold_in(_rk, 7), (32,), 0, max(1, 128 // 4) + 1, jnp.int32)
        _lenS2 = 128 - jax.random.randint(jax.random.fold_in(_rk, 8), (32,), 0, max(1, 128 // 4) + 1, jnp.int32)
        _ctx_1024P = jax.random.normal(jax.random.fold_in(_rk, 11), (32, 16, 128), jnp.float32)
        _ctx_1024c = jax.random.dirichlet(jax.random.fold_in(_rk, 511), 0.3 * jnp.ones((16,), jnp.float32), (32, 128))
        _ctx_1024t = jnp.einsum('bsk,bkd->bsd', _ctx_1024c, _ctx_1024P)
        _ctx_1024t = _ctx_1024t * jax.lax.rsqrt(jnp.mean(jnp.square(_ctx_1024t)) + 1e-12) * 0.953939
        ctx_1024 = -1.39393e-06 + 0.999914 * (_ctx_1024t + 0.3 * jax.random.normal(jax.random.fold_in(_rk, 611), (32, 128, 128), jnp.float32))
        return (x, ctx_1024)
    x, ctx_1024 = _rec_inputs()

    def _L0_attn_setup():
        import jax, jax.numpy as jnp
        import numpy as np
        D_MODEL = 128
        Q_HEADS = 16
        KV_HEADS = 4
        HEAD_DIM = D_MODEL // Q_HEADS
        KV_DIM = HEAD_DIM * KV_HEADS
        GROUPS = Q_HEADS // KV_HEADS
        LN_EPS = 1e-05
        NEG_INF = -10000000000.0
        key = jax.random.key(seed)
        ks = jax.random.split(key, 6)
        b, n = (2, 256)

        def xavier(k, fan_in, fan_out):
            limit = np.sqrt(6.0 / (fan_in + fan_out)).astype(np.float32)
            return jax.random.uniform(k, (fan_in, fan_out), jnp.float32, -limit, limit)
        return {'x': jax.random.normal(ks[0], (b, n, D_MODEL), jnp.float32), 'Wq': xavier(ks[1], D_MODEL, D_MODEL), 'bq': jnp.zeros((D_MODEL,), jnp.float32), 'Wk': xavier(ks[2], D_MODEL, KV_DIM), 'bk': jnp.zeros((KV_DIM,), jnp.float32), 'Wv': xavier(ks[3], D_MODEL, KV_DIM), 'bv': jnp.zeros((KV_DIM,), jnp.float32), 'ln_g': jnp.ones((D_MODEL,), jnp.float32), 'ln_b': jnp.zeros((D_MODEL,), jnp.float32), 'Wo': xavier(ks[4], D_MODEL, D_MODEL), 'bo': jnp.zeros((D_MODEL,), jnp.float32)}
    _L0_attn_all = _L0_attn_setup()
    _L0_attn_in = {k: v for k, v in _L0_attn_all.items() if k in ('Wq', 'bq', 'Wk', 'bk', 'Wv', 'bv', 'ln_g', 'ln_b', 'Wo', 'bo')}
    del _L0_attn_all

    def _L0_xattn_setup():
        import jax, jax.numpy as jnp
        import numpy as np
        HIDDEN = 128
        NUM_HEADS = 16
        HEAD_DIM = HIDDEN // NUM_HEADS
        EPS = 1e-05

        def rms_norm(x, weight, eps=EPS):
            var = jnp.mean(jnp.square(x), axis=-1, keepdims=True)
            return x * jax.lax.rsqrt(var + eps) * weight
        key = jax.random.key(seed)
        ks = jax.random.split(key, 9)
        B, Sq, Skv = (2, 256, 256)
        scale = 1.0 / np.sqrt(HIDDEN)
        q = jax.random.normal(ks[0], (B, Sq, HIDDEN), dtype=jnp.float32)
        kv = jax.random.normal(ks[1], (B, Skv, HIDDEN), dtype=jnp.float32)
        w_norm = jnp.ones((HIDDEN,), dtype=jnp.float32)
        w_q = jax.random.normal(ks[2], (HIDDEN, HIDDEN), dtype=jnp.float32) * scale
        b_q = jnp.zeros((HIDDEN,), dtype=jnp.float32)
        w_kv = jax.random.normal(ks[3], (2 * HIDDEN, HIDDEN), dtype=jnp.float32) * scale
        b_kv = jnp.zeros((2 * HIDDEN,), dtype=jnp.float32)
        w_out = jax.random.normal(ks[4], (HIDDEN, HIDDEN), dtype=jnp.float32) * scale
        b_out = jnp.zeros((HIDDEN,), dtype=jnp.float32)
        return {'q': q, 'kv': kv, 'w_norm': w_norm, 'w_q': w_q, 'b_q': b_q, 'w_kv': w_kv, 'b_kv': b_kv, 'w_out': w_out, 'b_out': b_out}
    _L0_xattn_all = _L0_xattn_setup()
    _L0_xattn_in = {k: v for k, v in _L0_xattn_all.items() if k in ('w_norm', 'w_q', 'b_q', 'w_kv', 'b_kv', 'w_out', 'b_out')}
    del _L0_xattn_all

    def _L0_ffn_setup():
        import jax, jax.numpy as jnp
        import numpy as np
        HID = 128
        NH = 16
        NKV = 4
        HD = HID // NH
        E = 8
        TOPK = 2
        FFN = 256
        EPS = 1e-05
        THETA = 10000.0

        def _rmsnorm(x, w):
            var = jnp.mean(x * x, axis=-1, keepdims=True)
            return x * jax.lax.rsqrt(var + EPS) * w

        def _rope_tables(S):
            inv_freq = 1.0 / THETA ** (jnp.arange(0, HD, 2, dtype=jnp.float32) / HD)
            freqs = jnp.arange(S, dtype=jnp.float32)[:, None] * inv_freq[None, :]
            emb = jnp.concatenate([freqs, freqs], axis=-1)
            return (jnp.cos(emb), jnp.sin(emb))

        def _apply_rope(t, cos, sin):
            t1, t2 = jnp.split(t, 2, axis=-1)
            rot = jnp.concatenate([-t2, t1], axis=-1)
            return t * cos[None, :, None, :] + rot * sin[None, :, None, :]
        key = jax.random.key(seed)
        ks = jax.random.split(key, 6)
        B, S = (1, 256)
        x = jax.random.normal(ks[0], (B, S, HID), dtype=jnp.float32)
        wqkv = jax.random.normal(ks[1], ((NH + 2 * NKV) * HD, HID), dtype=jnp.float32) * 0.02
        wo = jax.random.normal(ks[2], (HID, NH * HD), dtype=jnp.float32) * 0.02
        gate_w = jax.random.normal(ks[3], (E, HID), dtype=jnp.float32) * 0.02
        w13 = jax.random.normal(ks[4], (E, 2 * FFN, HID), dtype=jnp.float32) * 0.02
        w2 = jax.random.normal(ks[5], (E, HID, FFN), dtype=jnp.float32) * 0.02
        return {'x': x, 'ln1_w': jnp.ones((HID,), jnp.float32), 'ln2_w': jnp.ones((HID,), jnp.float32), 'wqkv': wqkv, 'wo': wo, 'gate_w': gate_w, 'w13': w13, 'w2': w2}
    _L0_ffn_all = _L0_ffn_setup()
    _L0_ffn_in = {k: v for k, v in _L0_ffn_all.items() if k in ('ln1_w', 'ln2_w', 'wqkv', 'wo', 'gate_w', 'w13', 'w2')}
    del _L0_ffn_all
    return {'x': x, 'ctx_1024': ctx_1024, 'L0_attn_Wq': _L0_attn_in['Wq'], 'L0_attn_bq': _L0_attn_in['bq'], 'L0_attn_Wk': _L0_attn_in['Wk'], 'L0_attn_bk': _L0_attn_in['bk'], 'L0_attn_Wv': _L0_attn_in['Wv'], 'L0_attn_bv': _L0_attn_in['bv'], 'L0_attn_ln_g': _L0_attn_in['ln_g'], 'L0_attn_ln_b': _L0_attn_in['ln_b'], 'L0_attn_Wo': _L0_attn_in['Wo'], 'L0_attn_bo': _L0_attn_in['bo'], 'L0_xattn_w_norm': _L0_xattn_in['w_norm'], 'L0_xattn_w_q': _L0_xattn_in['w_q'], 'L0_xattn_b_q': _L0_xattn_in['b_q'], 'L0_xattn_w_kv': _L0_xattn_in['w_kv'], 'L0_xattn_b_kv': _L0_xattn_in['b_kv'], 'L0_xattn_w_out': _L0_xattn_in['w_out'], 'L0_xattn_b_out': _L0_xattn_in['b_out'], 'L0_ffn_ln1_w': _L0_ffn_in['ln1_w'], 'L0_ffn_ln2_w': _L0_ffn_in['ln2_w'], 'L0_ffn_wqkv': _L0_ffn_in['wqkv'], 'L0_ffn_wo': _L0_ffn_in['wo'], 'L0_ffn_gate_w': _L0_ffn_in['gate_w'], 'L0_ffn_w13': _L0_ffn_in['w13'], 'L0_ffn_w2': _L0_ffn_in['w2']}

def reference(x, ctx_1024, L0_attn_Wq, L0_attn_bq, L0_attn_Wk, L0_attn_bk, L0_attn_Wv, L0_attn_bv, L0_attn_ln_g, L0_attn_ln_b, L0_attn_Wo, L0_attn_bo, L0_xattn_w_norm, L0_xattn_w_q, L0_xattn_b_q, L0_xattn_w_kv, L0_xattn_b_kv, L0_xattn_w_out, L0_xattn_b_out, L0_ffn_ln1_w, L0_ffn_ln2_w, L0_ffn_wqkv, L0_ffn_wo, L0_ffn_gate_w, L0_ffn_w13, L0_ffn_w2):
    import jax
    import jax.numpy as jnp

    def _L0_attn_ref(x, Wq, bq, Wk, bk, Wv, bv, ln_g, ln_b, Wo, bo):
        import jax, jax.numpy as jnp
        import numpy as np
        D_MODEL = 128
        Q_HEADS = 16
        KV_HEADS = 4
        HEAD_DIM = D_MODEL // Q_HEADS
        KV_DIM = HEAD_DIM * KV_HEADS
        GROUPS = Q_HEADS // KV_HEADS
        LN_EPS = 1e-05
        NEG_INF = -10000000000.0
        b, n, _ = x.shape
        q = x @ Wq + bq
        k = x @ Wk + bk
        v = x @ Wv + bv
        q = q.reshape(b, n, GROUPS, KV_HEADS, HEAD_DIM)
        q = jnp.transpose(q, (0, 2, 3, 1, 4))
        k = k.reshape(b, n, KV_HEADS, HEAD_DIM)
        v = v.reshape(b, n, KV_HEADS, HEAD_DIM)
        scale = jnp.asarray(HEAD_DIM ** 0.5, q.dtype)
        q = q / scale
        attn_logits = jnp.einsum('bghnd,bmhd->bghnm', q, k)
        causal = jnp.tril(jnp.ones((n, n), dtype=bool))
        attn_logits = jnp.where(causal[None, None, None, :, :], attn_logits, NEG_INF)
        attn = jax.nn.softmax(attn_logits, axis=-1)
        out = jnp.einsum('bghnm,bmhd->bghnd', attn, v)
        out = jnp.transpose(out, (0, 3, 1, 2, 4)).reshape(b, n, D_MODEL)
        mu = jnp.mean(out, axis=-1, keepdims=True)
        var = jnp.var(out, axis=-1, keepdims=True)
        out = (out - mu) * jax.lax.rsqrt(var + LN_EPS) * ln_g + ln_b
        out = out @ Wo + bo
        return out

    def _L0_xattn_ref(q, kv, w_norm, w_q, b_q, w_kv, b_kv, w_out, b_out):
        import jax, jax.numpy as jnp
        import numpy as np
        HIDDEN = 128
        NUM_HEADS = 16
        HEAD_DIM = HIDDEN // NUM_HEADS
        EPS = 1e-05

        def rms_norm(x, weight, eps=EPS):
            var = jnp.mean(jnp.square(x), axis=-1, keepdims=True)
            return x * jax.lax.rsqrt(var + eps) * weight
        qn = rms_norm(q, w_norm)
        qp = qn @ w_q.T + b_q
        kvp = kv @ w_kv.T + b_kv
        k, v = jnp.split(kvp, 2, axis=-1)
        B, Sq, _ = qp.shape
        Skv = k.shape[1]
        qh = qp.reshape(B, Sq, NUM_HEADS, HEAD_DIM).transpose(0, 2, 1, 3)
        kh = k.reshape(B, Skv, NUM_HEADS, HEAD_DIM).transpose(0, 2, 1, 3)
        vh = v.reshape(B, Skv, NUM_HEADS, HEAD_DIM).transpose(0, 2, 1, 3)
        scores = jnp.einsum('bhqd,bhkd->bhqk', qh, kh) * HEAD_DIM ** (-0.5)
        attn = jax.nn.softmax(scores, axis=-1)
        o = jnp.einsum('bhqk,bhkd->bhqd', attn, vh)
        o = o.transpose(0, 2, 1, 3).reshape(B, Sq, HIDDEN)
        return o @ w_out.T + b_out

    def _L0_ffn_ref(x, ln1_w, ln2_w, wqkv, wo, gate_w, w13, w2):
        import jax, jax.numpy as jnp
        import numpy as np
        HID = 128
        NH = 16
        NKV = 4
        HD = HID // NH
        E = 8
        TOPK = 2
        FFN = 256
        EPS = 1e-05
        THETA = 10000.0

        def _rmsnorm(x, w):
            var = jnp.mean(x * x, axis=-1, keepdims=True)
            return x * jax.lax.rsqrt(var + EPS) * w

        def _rope_tables(S):
            inv_freq = 1.0 / THETA ** (jnp.arange(0, HD, 2, dtype=jnp.float32) / HD)
            freqs = jnp.arange(S, dtype=jnp.float32)[:, None] * inv_freq[None, :]
            emb = jnp.concatenate([freqs, freqs], axis=-1)
            return (jnp.cos(emb), jnp.sin(emb))

        def _apply_rope(t, cos, sin):
            t1, t2 = jnp.split(t, 2, axis=-1)
            rot = jnp.concatenate([-t2, t1], axis=-1)
            return t * cos[None, :, None, :] + rot * sin[None, :, None, :]
        B, S, _ = x.shape
        h = _rmsnorm(x, ln1_w)
        qkv = jnp.einsum('bsh,oh->bso', h, wqkv)
        q = qkv[..., :NH * HD].reshape(B, S, NH, HD)
        k = qkv[..., NH * HD:(NH + NKV) * HD].reshape(B, S, NKV, HD)
        v = qkv[..., (NH + NKV) * HD:].reshape(B, S, NKV, HD)
        cos, sin = _rope_tables(S)
        q = _apply_rope(q, cos, sin)
        k = _apply_rope(k, cos, sin)
        groups = NH // NKV
        k = jnp.repeat(k, groups, axis=2)
        v = jnp.repeat(v, groups, axis=2)
        scale = HD ** (-0.5)
        scores = jnp.einsum('bqhd,bkhd->bhqk', q, k) * scale
        causal = jnp.tril(jnp.ones((S, S), dtype=bool))
        scores = jnp.where(causal[None, None], scores, jnp.finfo(scores.dtype).min)
        probs = jax.nn.softmax(scores, axis=-1)
        attn = jnp.einsum('bhqk,bkhd->bqhd', probs, v).reshape(B, S, NH * HD)
        x = x + jnp.einsum('bso,ho->bsh', attn, wo)
        h = _rmsnorm(x, ln2_w).reshape(-1, HID)
        T = h.shape[0]
        logits = jnp.einsum('th,eh->te', h, gate_w)
        rprobs = jax.nn.softmax(logits.astype(jnp.float32), axis=-1)
        topw, topi = jax.lax.top_k(rprobs, TOPK)
        topw = topw / jnp.sum(topw, axis=-1, keepdims=True)
        wfull = jnp.zeros((T, E), jnp.float32).at[jnp.arange(T)[:, None], topi].set(topw)
        wfull = wfull.astype(h.dtype)
        out = jnp.zeros((T, HID), h.dtype)
        for e in range(E):
            w1 = w13[e, :FFN]
            w3 = w13[e, FFN:]
            g = jax.nn.silu(h @ w1.T) * (h @ w3.T)
            out = out + jnp.einsum('tf,hf->th', g, w2[e]) * wfull[:, e:e + 1]
        return x + out.reshape(B, S, HID)
    x = _layernorm(x + _L0_attn_ref(x, L0_attn_Wq, L0_attn_bq, L0_attn_Wk, L0_attn_bk, L0_attn_Wv, L0_attn_bv, L0_attn_ln_g, L0_attn_ln_b, L0_attn_Wo, L0_attn_bo), axis=-1)
    x = _layernorm(x + _L0_xattn_ref(x, ctx_1024, L0_xattn_w_norm, L0_xattn_w_q, L0_xattn_b_q, L0_xattn_w_kv, L0_xattn_b_kv, L0_xattn_w_out, L0_xattn_b_out), axis=-1)
    x = _layernorm(x + _L0_ffn_ref(x, L0_ffn_ln1_w, L0_ffn_ln2_w, L0_ffn_wqkv, L0_ffn_wo, L0_ffn_gate_w, L0_ffn_w13, L0_ffn_w2), axis=-1)
    return x

_drawn_inputs = setup_inputs


def setup_inputs(seed=0):
    import zlib

    import numpy as np

    out = dict(_drawn_inputs(seed))
    spreads = {'L0_attn_bq': (0.0, 0.1),
     'L0_attn_bk': (0.0, 0.8),
     'L0_attn_bv': (0.0, 0.1),
     'L0_attn_ln_g': (1.0, 0.2),
     'L0_attn_ln_b': (0.0, 0.1),
     'L0_attn_bo': (0.0, 0.1),
     'L0_xattn_w_norm': (1.0, 0.2),
     'L0_xattn_b_q': (0.0, 0.386),
     'L0_xattn_b_kv': (0.0, 0.1),
     'L0_xattn_b_out': (0.0, 0.1),
     'L0_ffn_ln1_w': (1.0, 0.6),
     'L0_ffn_ln2_w': (1.0, 0.6)}
    factors = {'L0_ffn_wqkv': 3.573,
     'L0_ffn_wo': 3.407,
     'L0_ffn_gate_w': 8.0,
     'L0_ffn_w13': 8.0,
     'L0_ffn_w2': 8.0}
    for name, (base, spread) in spreads.items():
        noise = np.random.default_rng([zlib.crc32(name.encode()), seed]).standard_normal(out[name].shape)
        drawn = base * np.exp(spread * noise) if base else spread * noise
        out[name] = jnp.asarray(drawn.astype(out[name].dtype))
    for name, factor in factors.items():
        out[name] = (out[name] * factor).astype(out[name].dtype)
    return out
```

```python
from contextlib import ExitStack

import concourse.bass as bass
from concourse import mybir

P = 128
F32 = mybir.dt.float32
F32R = mybir.dt.float32r
BF16 = mybir.dt.bfloat16
U32 = mybir.dt.uint32
ALU = mybir.AluOpType
ACT = mybir.ActivationFunctionType
AX = mybir.AxisListType

HD = 8
SLOT = 32
NEG = -1e30
EPS = 1e-5
SCALE = HD ** -0.5
STREAMS = 4
KINDS = 3
STEPS = STREAMS * KINDS
SELF, CROSS, ROPE = range(KINDS)


def kind_of(n):
    return (n % STEPS) // STREAMS


def program(nc, x, ctx_in, w_self, w_crossq, w_crosskv, w_rope, w_out, bias_rows, feat_cols, tables, ident_in,
            mask_in, gate_in, w13_in, w2_in, out):
    NB = x.shape[0]
    ITER = NB // STREAMS
    E = gate_in.shape[1]
    F = w13_in.shape[1] // (2 * E)
    FC = F // P
    N = STREAMS * P

    with ExitStack() as ctx:
        def sb(name, shape, dt=F32):
            return ctx.enter_context(nc.sbuf_tensor(name, shape, dt))

        def ps(name):
            return ctx.enter_context(nc.psum_tensor(name, [P, 512], F32))

        def sem(name):
            return ctx.enter_context(nc.semaphore(name))

        Wself = sb("Wself", [P, 192])
        Wcq = sb("Wcq", [P, P])
        Wckv = sb("Wckv", [P, 2 * P])
        Wrope = sb("Wrope", [P, 192])
        Wout = sb("Wout", [P, KINDS, P])
        bias = sb("bias", [P, 832])
        b_self, b_cross = bias[:, 0:192], bias[:, 192:576]
        b_out = [bias[:, 576:704], bias[:, 704:832]]
        feat = sb("feat", [P, 5])
        ln_g, ln_b, norm_x, norm_1, norm_2 = [feat[:, k:k + 1] for k in range(5)]
        tab = sb("tab", [P, 4 + 4 + 8 + 8 + 4 + 4 + 8 + 1 + 1])
        same_c, same_r, cos_t, sin_t = tab[:, 0:4], tab[:, 4:8], tab[:, 8:16], tab[:, 16:24]
        slot3_one, cross_one, iota_e, minus_half, eps_col = tab[:, 24:28], tab[:, 28:32], tab[:, 32:40], tab[:, 40:41], tab[:, 41:42]
        ident = sb("ident", [P, P])
        ident_b = sb("ident_b", [P, P], BF16)
        mask_f = sb("mask_f", [P, P])
        mask_b = sb("mask_b", [P, 4, P], BF16)
        ones_r = sb("ones_r", [P, 4, P], F32R)
        ones_f = sb("ones_f", [P, P])
        gate_f = sb("gate_f", [P, E])
        gate_r = sb("gate_r", [P, 2, E], F32R)
        w13_f = sb("w13_f", [P, 2 * E * F])
        w13_hi = sb("w13_hi", [P, 2 * E * F], F32R)
        w13_lo = sb("w13_lo", [P, 2 * E * F], F32R)
        w2_f = sb("w2_f", [P, E * FC * P])

        XL = [sb(f"XL{j}", [P, P]) for j in range(STREAMS)]
        CL = [sb(f"CL{j}", [P, P]) for j in range(STREAMS)]
        XS = [sb(f"XS{j}", [P, P]) for j in range(STREAMS)]
        H = [sb(f"H{j}", [P, P]) for j in range(STREAMS)]
        XB = [sb(f"XB{j}", [P, P]) for j in range(STREAMS)]
        xTs = sb("xTs", [P, P])
        cTs = sb("cTs", [P, P])
        T = sb("T", [P, 2 * P])
        T3 = sb("T3", [P, 5, 3, SLOT])
        rope1 = sb("rope1", [P, 20, HD])
        rope2 = sb("rope2", [P, 20, HD])
        VG = [sb(f"VG{b}", [P, 4, SLOT]) for b in range(3)]
        VC = [sb(f"VC{b}", [P, 16, SLOT]) for b in range(3)]
        Qs = [sb(f"Qs{b}", [P, 512], F32R) for b in range(2)]
        K1 = sb("K1", [P, P], F32R)
        Kz = [sb(f"Kz{b}", [P, 4, P], F32R) for b in range(2)]
        c_hi = sb("c_hi", [P, 2, P], F32R)
        c_lo = sb("c_lo", [P, 2, P], F32R)
        Qhi = [sb(f"Qhi{b}", [P, 4, P], F32R) for b in range(2)]
        Qlo = [sb(f"Qlo{b}", [P, 4, P], F32R) for b in range(2)]
        Khi = [sb(f"Khi{b}", [P, 4, P], F32R) for b in range(2)]
        Klo = [sb(f"Klo{b}", [P, 4, P], F32R) for b in range(2)]
        Mbd = [sb(f"Mbd{b}", [P, 4, P], F32R) for b in range(2)]
        negmax = sb("negmax", [P, 4, 4])
        MxG = sb("MxG", [P, 4, P])
        MxC = sb("MxC", [P, 16, HD])
        PT = [sb(f"PT{c}", [P, 512]) for c in range(4)]
        OTs = sb("OTs", [P, 512])
        rec = sb("rec", [P, 4, 4])
        On = sb("On", [P, P])
        On2 = sb("On2", [P, P])
        OnT = sb("OnT", [P, P])
        R = sb("R", [P, P])
        st_in = sb("st_in", [P, 6])
        mv_in = sb("mv_in", [P, 2])
        rs_in = sb("rs_in", [P, 2])
        st_post = sb("st_post", [P, 6])
        mv_post = sb("mv_post", [P, 2])
        rs_post = sb("rs_post", [P, 6])
        X3 = sb("X3", [P, NB * P])
        X23 = sb("X23", [P, NB * P])

        st4 = sb("st4", [P, 4, 6])
        mv4 = sb("mv4", [P, 4, 2])
        q4 = sb("q4", [P, 4, 2])
        rs4 = sb("rs4", [P, 4, 1])
        H2 = sb("h_moe", [P, 4, P])
        hT_hi = [sb(f"hT_hi{b}", [P, N], F32R) for b in range(2)]
        hT_lo = [sb(f"hT_lo{b}", [P, N], F32R) for b in range(2)]
        lg = sb("lg", [P, 4, E])
        top8 = sb("top8", [P, 4, 8])
        idx8 = sb("idx8", [P, 4, 8], U32)
        idxf = sb("idxf", [P, 4, 8])
        neg_top = sb("neg_top", [P, 4, 1])
        lg2 = sb("lg2", [P, 4, E])
        ex = sb("ex", [P, 4, E])
        hot = sb("hot", [P, 4, E])
        hot2 = sb("hot2", [P, 4, E])
        wsum = sb("wsum", [P, 4, 1])
        wrec = sb("wrec", [P, 4, 1])
        Wr = [sb(f"Wr{b}", [P, 4, E]) for b in range(2)]
        th = [sb(f"th{b}", [P, N]) for b in range(2)]
        sg = [sb(f"sg{b}", [P, N]) for b in range(2)]
        G = PT
        yw = [sb(f"yw{b}", [P, 4, P]) for b in range(2)]
        acc = [sb(f"acc{b}", [P, 4, P]) for b in range(2)]
        st_f = sb("st_f", [P, 4, 6])
        mv_f = sb("mv_f", [P, 4, 2])
        rs_f = sb("rs_f", [P, 4, 2])
        fin = [sb(f"fin{b}", [P, 4, P]) for b in range(2)]

        bA, bQ, bC, bS0, bS1, bT0, bT1, bO = [ps(f"bank{k}") for k in range(8)]
        bS, bT = [bS0, bS1], [bT0, bT1]

        w_ld = sem("w_ld")
        x_ld = [sem(f"x_ld{j}") for j in range(STREAMS)]
        c_ld = [sem(f"c_ld{j}") for j in range(STREAMS)]
        w13_ld = sem("w13_ld")
        init_pool = sem("init_pool")
        init_dve = sem("init_dve")
        init_act = sem("init_act")
        waits_carried = sem("waits_carried")

        W_ALL = 16 * 11
        per_step = {}

        def step_sem(name, *counts):
            s = sem(name)
            per_step[s] = counts if len(counts) > 1 else counts * KINDS
            return s

        xT_done = step_sem("xT_done", 1)
        xT_evac = step_sem("xT_evac", 1)
        qkv_done = step_sem("qkv_done", 1)
        tok = step_sem("tok", 1, 1, 4)
        qkT_done = step_sem("qkT_done", 1)
        hi_done = step_sem("hi_done", 1)
        lo_done = step_sem("lo_done", 1)
        kz_done = step_sem("kz_done", 1)
        kz_pool = step_sem("kz_pool", 0, 1, 0)
        s_done = step_sem("s_done", 4)
        s_max = step_sem("s_max", 4)
        m_hi = step_sem("m_hi", 1)
        m_done = step_sem("m_done", 1)
        mT_done = step_sem("mT_done", 1)
        m_evac = step_sem("m_evac", 1)
        st_done = step_sem("st_done", 4)
        exp_done = step_sem("exp_done", 4)
        causal = step_sem("causal", 4, 0, 4)
        pv_done = step_sem("pv_done", 1)
        ot_evac = step_sem("ot_evac", 1)
        on_done = step_sem("on_done", 1)
        c_dve = step_sem("c_dve", 4, 1, 1)
        ln_in = step_sem("ln_in", 2, 0, 0)
        o_ready = step_sem("o_ready", 1)
        oT_done = step_sem("oT_done", 1)
        oT_evac = step_sem("oT_evac", 1)
        y_done = step_sem("y_done", 1)
        xb_done = step_sem("xb_done", 1)
        res = step_sem("res", 1)
        post = step_sem("post", 2, 2, 0)
        ln_post = step_sem("ln_post", 6, 6, 0)
        xs_done = step_sem("xs_done", 1, 1, 0)
        h_done = step_sem("h_done", 1, 1, 0)

        def level(s, i, n, m=None):
            counts = per_step[s]
            i, n = i + n // STEPS, n % STEPS
            if m is None:
                m = counts[kind_of(n)]
            return i * STREAMS * sum(counts) + sum(counts[kind_of(a)] for a in range(n)) + m

        def exists(i, n):
            if not isinstance(i, int):
                return True
            return 0 <= i * STEPS + n < ITER * STEPS

        def v3(ap, b):
            return ap.rearrange("p (a b) -> p a b", b=b)

        def rep(ap, k):
            return ap.unsqueeze(1).to_broadcast([ap.shape[0], k, ap.shape[1]])

        def last(ap, k):
            return ap.unsqueeze(2).to_broadcast([ap.shape[0], ap.shape[1], k])

        def thrice(ap):
            return v3(ap, SLOT).unsqueeze(2).to_broadcast([P, 5, 3, SLOT])

        block = ctx.enter_context(nc.Block())

        per_group = {}

        def p2(name, per_iter):
            s = sem(name)
            per_group[s] = per_iter
            return s

        w13_split = sem("w13_split")
        n_units = E * FC
        pre_st = p2("pre_st", 5)
        pre_q = p2("pre_q", 1)
        pre_rs = p2("pre_rs", 1)
        pre_h = p2("pre_h", 4)
        pre_t = p2("pre_t", 1)
        pre_hi = p2("pre_hi", 1)
        pre_lo = p2("pre_lo", 1)
        pre_g = p2("pre_g", 1)
        rt = p2("rt", 17)
        rt_exp = p2("rt_exp", 1)
        xu_done = p2("xu_done", n_units)
        tanh_done = p2("tanh_done", n_units)
        sg_done = p2("sg_done", n_units)
        g_done = p2("g_done", n_units)
        y2_done = p2("y2_done", E)
        yw_done = p2("yw_done", E)
        acc_done = p2("acc_done", E)
        fin_st = p2("fin_st", 5)
        fin_rs = p2("fin_rs", 2)
        fin_done = p2("fin_done", 4)
        wr_done = p2("wr_done", 1)
        pre_pool = p2("pre_pool", 2)
        pool_zero = sem("pool_zero")
        out_done = [sem(f"out_done{b}") for b in range(2)]

        def level2(s, i, m):
            return i * per_group[s] + m

        def past(i, k):
            return not isinstance(i, int) or i > 0 or k >= 0

        @block.sync
        def _(sp):
            def load(i, which):
                for j in range(STREAMS):
                    b = i * STREAMS + j
                    if which == "x":
                        if not (isinstance(i, int) and i == 0):
                            sp.wait_ge(xT_done, level(xT_done, i - 1, j))
                            sp.sem_inc(waits_carried, 1)
                            sp.wait_ge(xb_done, level(xb_done, i - 1, j))
                            sp.sem_inc(waits_carried, 1)
                        sp.dma_start(XL[j][:, :], x[bass.ds(b, 1), :, :].rearrange("b s d -> (b s) d")
                                     ).then_inc(x_ld[j], 16)
                    else:
                        if not (isinstance(i, int) and i == 0):
                            sp.wait_ge(xT_done, level(xT_done, i - 1, STREAMS + j))
                            sp.sem_inc(waits_carried, 1)
                        sp.dma_start(CL[j][:, :], ctx_in[bass.ds(b, 1), :, :].rearrange("b s d -> (b s) d")
                                     ).then_inc(c_ld[j], 16)

            sp.dma_start(ident[:, :], ident_in).then_inc(w_ld, 16)
            sp.dma_start(XL[0][:, :], x[0, :, :]).then_inc(x_ld[0], 16)
            sp.dma_start(Wself[:, :], w_self).then_inc(w_ld, 16)
            sp.dma_start(tab[:, :], tables).then_inc(w_ld, 16)
            sp.dma_start(bias[:, :], bias_rows).then_inc(w_ld, 16)
            sp.dma_start(mask_f[:, :], mask_in).then_inc(w_ld, 16)
            sp.dma_start(feat[:, :], feat_cols).then_inc(w_ld, 16)
            sp.dma_start(Wout[:, :, :], w_out.rearrange("k p n -> p k n")).then_inc(w_ld, 16)
            sp.dma_start(Wcq[:, :], w_crossq).then_inc(w_ld, 16)
            sp.dma_start(Wckv[:, :], w_crosskv).then_inc(w_ld, 16)
            sp.dma_start(Wrope[:, :], w_rope).then_inc(w_ld, 16)
            sp.dma_start(gate_f[:, :], gate_in).then_inc(w_ld, 16)
            for j in range(1, STREAMS):
                sp.dma_start(XL[j][:, :], x[j, :, :]).then_inc(x_ld[j], 16)
            load(0, "c")
            sp.dma_start(w13_f[:, :], w13_in).then_inc(w13_ld, 16)
            sp.dma_start(w2_f[:, :], w2_in).then_inc(w13_ld, 16)
            with sp.Fori(1, ITER) as i:
                load(i, "x")
                load(i, "c")

            def store(i, b):
                sp.wait_ge(fin_done, level2(fin_done, i, 4))
                sp.sem_inc(waits_carried, 1)
                sp.dma_start(out[bass.ds(i * STREAMS, STREAMS), :, :].rearrange("b s d -> s b d"),
                             fin[b][:, :, :]).then_inc(out_done[b], 16)

            with sp.Fori(0, ITER // 2) as h:
                for b in range(2):
                    store(h * 2 + b, b)
            for b in range(2):
                sp.wait_ge(out_done[b], 16 * (ITER // 2))


        def run_slots(eng, slot):
            for n in range(STEPS):
                slot(0, n)
            with eng.Fori(1, ITER) as i:
                for n in range(STEPS):
                    slot(i, n)
            for n in range(3):
                slot(ITER, n)

        def run_groups(eng, body):
            body(0, 0, True)
            body(1, 1, True)
            with eng.Fori(1, ITER // 2 - 1) as h:
                body(h * 2, 0, True)
                body(h * 2 + 1, 1, True)
            body(ITER - 2, 0, True)
            body(ITER - 1, 1, False)

        INIT_POOL = 1
        INIT_DVE = 1


        @block.tensor
        def _(pe):
            mm = nc.tensor.matmul

            def A1(i, n):
                k, j = kind_of(n), n % STREAMS
                if k == SELF:
                    pe.wait_ge(x_ld[j], 16 * (i + 1))
                else:
                    pe.wait_ge(h_done, level(h_done, i, n - STREAMS))
                if exists(i, n - 1):
                    pe.wait_ge(lo_done, level(lo_done, i, n - 1))
                src = XL[j] if k == SELF else H[j]
                t = nc.tensor.transpose(bA[:, 0:P], src[:, :], ident[:, :])
                if k == CROSS:
                    pe.wait_ge(c_ld[j], 16 * (i + 1))
                    t = nc.tensor.transpose(bA[:, 2 * P:3 * P], CL[j][:, :], ident[:, :])
                t.then_inc(xT_done, 1)

            def A2(i, n):
                k = kind_of(n)
                pe.wait_ge(xT_evac, level(xT_evac, i, n))
                if k == CROSS:
                    mm(bA[:, P:2 * P], xTs[:, :], Wcq[:, :], start=True, stop=True)
                    t = mm(bA[:, 2 * P:4 * P], cTs[:, :], Wckv[:, :], start=True, stop=True)
                else:
                    t = mm(bA[:, P:P + 192], xTs[:, :], (Wself if k == SELF else Wrope)[:, :], start=True, stop=True)
                t.then_inc(qkv_done, 1)

            def A3(i, n):
                k = kind_of(n)
                pe.wait_ge(tok, level(tok, i, n))
                if exists(i, n - 2):
                    pe.wait_ge(m_evac, level(m_evac, i, n - 2))
                if k == CROSS:
                    nc.tensor.transpose(bQ[:, 0:P], T[:, 0:P], ident[:, :])
                    t = nc.tensor.transpose(bA[:, 0:P], T[:, P:2 * P], ident[:, :])
                else:
                    for g in range(4):
                        nc.tensor.transpose(bQ[0:96, P * g:P * g + P], T3[:, g, :, :], ident[:, :])
                    t = nc.tensor.transpose(bA[0:96, 0:P], T3[:, 4, :, :], ident[:, :])
                t.then_inc(qkT_done, 1)

            def A4(i, n, gs):
                k, b = kind_of(n), n % 2
                if 0 in gs:
                    pe.wait_ge(kz_done, level(kz_done, i, n))
                for g in gs:
                    if exists(i, n - 1) or g >= 2:
                        pe.wait_ge(s_max, level(s_max, i, n, g - 1))
                    if k == CROSS:
                        t = mm(bS[g % 2][:, :], Qhi[b][:, g, :], Khi[b][:, :, :], start=True, stop=True)
                    else:
                        mm(bS[g % 2][:, :], Qs[b][0:96, P * g:P * g + P], Kz[b][0:96, :, :], start=True, stop=False)
                        t = mm(bS[g % 2][:, :], ident_b[:, :], mask_b[:, :, :], start=False, stop=True)
                    t.then_inc(s_done, 1)

            def A5(i, n):
                k = kind_of(n)
                pe.wait_ge(m_done, level(m_done, i, n))
                if exists(i, n + 1):
                    pe.wait_ge(lo_done, level(lo_done, i, n + 1))
                if k == CROSS:
                    t = nc.tensor.transpose(bQ[:, 0:P], MxC[:, :, :], ident[:, :])
                else:
                    for g in range(4):
                        t = nc.tensor.transpose(v3(bQ[:, :], P)[:, g, :], MxG[:, g, :], ident[:, :])
                t.then_inc(mT_done, 1)

            def B1(i, n, cs):
                k, b = kind_of(n), n % 2
                if 0 in cs:
                    pe.wait_ge(m_evac, level(m_evac, i, n))
                    if k == CROSS:
                        pe.wait_ge(kz_pool, level(kz_pool, i, n))
                for c in cs:
                    if exists(i, n - 1) or c >= 2:
                        pe.wait_ge(exp_done, level(exp_done, i, n, c - 1))
                    o = bT[c % 2][:, :]
                    if k == CROSS:
                        mm(o, Khi[b][:, c, :], Qhi[b][:, :, :], start=True, stop=False)
                        mm(o, Khi[b][:, c, :], Qlo[b][:, :, :], start=False, stop=False)
                        mm(o, Klo[b][:, c, :], Qhi[b][:, :, :], start=False, stop=False)
                        t = mm(o, ones_r[:, c, :], Mbd[b][:, :, :], start=False, stop=True)
                    else:
                        t = mm(o, Kz[b][:, c, :], Qs[b][:, :], start=True, stop=True)
                    t.then_inc(st_done, 1)

            def B2(i, n):
                k, b = kind_of(n), n % 2
                if exists(i, n - 1):
                    pe.wait_ge(ot_evac, level(ot_evac, i, n - 1))
                for c in range(4):
                    if k == CROSS:
                        pe.wait_ge(exp_done, level(exp_done, i, n, c + 1))
                        for h in range(4):
                            t = mm(bO[SLOT * h:SLOT * h + SLOT, P * c:P * c + P], VC[n % 3][:, 4 * c + h, :],
                                   PT[c][:, P * h:P * h + P], start=True, stop=True, tile_position=(0, SLOT * h))
                    else:
                        pe.wait_ge(causal, level(causal, i, n, c + 1))
                        t = mm(bO[SLOT * c:SLOT * c + SLOT, :], VG[n % 3][:, c, :], PT[c][:, :], start=True, stop=True,
                               tile_position=(0, SLOT * c))
                t.then_inc(pv_done, 1)

            def C1(i, n):
                pe.wait_ge(ot_evac, level(ot_evac, i, n))
                if exists(i, n - 1):
                    pe.wait_ge(res, level(res, i, n - 1))
                for g in range(4):
                    t = nc.tensor.transpose(v3(bC[:, :], P)[:, g, :], OTs[:, P * g:P * g + P], ident[:, :])
                t.then_inc(on_done, 1)

            def C2(i, n):
                pe.wait_ge(o_ready, level(o_ready, i, n))
                t = nc.tensor.transpose(bC[:, 0:P], (On2 if kind_of(n) == SELF else On)[:, :], ident[:, :])
                t.then_inc(oT_done, 1)

            def C3(i, n):
                pe.wait_ge(oT_evac, level(oT_evac, i, n))
                mm(bC[:, P:2 * P], OnT[:, :], Wout[:, kind_of(n), :], start=True, stop=True).then_inc(y_done, 1)

            def slot(i, n):
                a, b, c = exists(i, n), exists(i, n - 1), exists(i, n - 2)
                if a:
                    A1(i, n)
                if c:
                    B1(i, n - 2, [2])
                if b:
                    A4(i, n - 1, [2])
                if a:
                    A2(i, n)
                if c:
                    B1(i, n - 2, [3])
                if b:
                    A4(i, n - 1, [3])
                if a:
                    A3(i, n)
                if c:
                    B2(i, n - 2)
                if b:
                    A5(i, n - 1)
                if c:
                    C1(i, n - 2)
                if a:
                    A4(i, n, [0, 1])
                if b:
                    B1(i, n - 1, [0, 1])
                if c:
                    C2(i, n - 2)
                    C3(i, n - 2)

            pe.wait_ge(w_ld, W_ALL)
            pe.wait_ge(init_pool, INIT_POOL)
            pe.wait_ge(init_dve, INIT_DVE)
            run_slots(pe, slot)

            def pre(i):
                pe.wait_ge(pre_h, level2(pre_h, i, 4))
                for t4 in range(4):
                    t = nc.tensor.transpose(v3(bQ[:, :], P)[:, t4, :], H2[:, t4, :], ident[:, :])
                t.then_inc(pre_t, 1)

            def router(i, b):
                pe.wait_ge(pre_lo, level2(pre_lo, i, 1))
                for t4 in range(4):
                    o = bC[:, E * t4:E * t4 + E]
                    lh, ll = hT_hi[b][:, P * t4:P * t4 + P], hT_lo[b][:, P * t4:P * t4 + P]
                    mm(o, lh, gate_r[:, 0, :], start=True, stop=False)
                    mm(o, lh, gate_r[:, 1, :], start=False, stop=False)
                    t = mm(o, ll, gate_r[:, 0, :], start=False, stop=True)
                t.then_inc(pre_g, 1)

            def unit(i, b, u):
                e, f = u // FC, u % FC
                for w in range(2):
                    o = (bS if w == 0 else bT)[u % 2][:, :]
                    if w == 0:
                        if past(i, u - 2):
                            pe.wait_ge(g_done, level2(g_done, i, u - 1))
                    col = (2 * e + w) * F + f * P
                    mm(o, w13_hi[:, col:col + P], hT_hi[b][:, :], start=True, stop=False)
                    mm(o, w13_hi[:, col:col + P], hT_lo[b][:, :], start=False, stop=False)
                    t = mm(o, w13_lo[:, col:col + P], hT_hi[b][:, :], start=False, stop=True)
                t.then_inc(xu_done, 1)

            def down(i, e):
                y = (bA, bO)[e % 2]
                pe.wait_ge(g_done, level2(g_done, i, FC * (e + 1)))
                if past(i, e - 2):
                    pe.wait_ge(yw_done, level2(yw_done, i, e - 1))
                for t4 in range(4):
                    for f in range(FC):
                        t = mm(y[:, P * t4:P * t4 + P], G[(FC * e + f) % 4][:, P * t4:P * t4 + P],
                               w2_f[:, (e * FC + f) * P:(e * FC + f + 1) * P], start=(f == 0), stop=(f == FC - 1))
                t.then_inc(y2_done, 1)

            def experts(i, b, more):
                for u in range(n_units):
                    unit(i, b, u)
                    if u % FC == 0 and u >= FC:
                        down(i, u // FC - 1)
                    if more and u == 5:
                        pre(i + 1)
                    if more and u == 7:
                        router(i + 1, 1 - b)
                down(i, E - 1)

            pe.wait_ge(w13_ld, 32)
            pe.wait_ge(w13_split, 2)
            pre(0)
            router(0, 0)
            run_groups(pe, experts)

        @block.scalar
        def _(act):
            def cp(out_, in_, **kw):
                return nc.scalar.activation(out_, in_, ACT.Identity if kw else ACT.Copy, **kw)

            def A1(i, n):
                k = kind_of(n)
                act.wait_ge(xT_done, level(xT_done, i, n))
                if k == SELF:
                    t = cp(xTs[:, :], bA[:, 0:P])
                elif k == CROSS:
                    cp(xTs[:, :], bA[:, 0:P], scale=norm_x)
                    t = cp(cTs[:, :], bA[:, 2 * P:3 * P])
                else:
                    t = cp(xTs[:, :], bA[:, 0:P], scale=norm_1)
                t.then_inc(xT_evac, 1)

            def A3(i, n):
                k, b = kind_of(n), n % 2
                act.wait_ge(qkT_done, level(qkT_done, i, n))
                if k == CROSS:
                    cp(c_hi[:, 0, :], bQ[:, 0:P])
                    t = cp(c_hi[:, 1, :], bA[:, 0:P])
                else:
                    cp(Qs[b][0:96, :], bQ[0:96, :])
                    t = cp(K1[0:96, :], bA[0:96, 0:P])
                t.then_inc(hi_done, 1)

            def A5(i, n):
                if kind_of(n) != CROSS:
                    act.wait_ge(mT_done, level(mT_done, i, n))
                    cp(Qs[n % 2][96:128, :], bQ[96:128, :]).then_inc(m_evac, 1)

            def B1(i, n, cs):
                for c in cs:
                    act.wait_ge(st_done, level(st_done, i, n, c + 1))
                    nc.scalar.activation(PT[c][:, :], bT[c % 2][:, :], ACT.Exp, scale=SCALE).then_inc(exp_done, 1)

            def B2(i, n):
                act.wait_ge(pv_done, level(pv_done, i, n))
                cp(OTs[:, :], bO[:, :]).then_inc(ot_evac, 1)

            def C2(i, n):
                act.wait_ge(oT_done, level(oT_done, i, n))
                kw = dict(scale=ln_g, bias=ln_b) if kind_of(n) == SELF else {}
                cp(OnT[:, :], bC[:, 0:P], **kw).then_inc(oT_evac, 1)

            def slot(i, n):
                a, b, c = exists(i, n), exists(i, n - 1), exists(i, n - 2)
                if a:
                    A1(i, n)
                if c:
                    B1(i, n - 2, [2, 3])
                if a:
                    A3(i, n)
                if c:
                    B2(i, n - 2)
                if b:
                    A5(i, n - 1)
                    B1(i, n - 1, [0, 1])
                if c:
                    C2(i, n - 2)

            act.wait_ge(w_ld, W_ALL)
            run_slots(act, slot)

            act.wait_ge(w13_ld, 32)
            half = E * F
            for q in range(2):
                cp(w13_hi[:, half * q:half * q + half], w13_f[:, half * q:half * q + half]).then_inc(init_act, 1)

            def pre(i, b):
                act.wait_ge(pre_t, level2(pre_t, i, 1))
                cp(hT_hi[b][:, :], bQ[:, :], scale=norm_2).then_inc(pre_hi, 1)

            def route(i):
                act.wait_ge(rt, level2(rt, i, 10))
                nc.scalar.activation(ex[:, :, :], lg2[:, :, :], ACT.Exp).then_inc(rt_exp, 1)

            def experts(i, b, more):
                for u in range(n_units):
                    act.wait_ge(xu_done, level2(xu_done, i, u + 1))
                    if past(i, u - 2):
                        act.wait_ge(sg_done, level2(sg_done, i, u - 1))
                    nc.scalar.activation(th[u % 2][:, :], bS[u % 2][:, :], ACT.Tanh, scale=0.5).then_inc(tanh_done, 1)
                    if more and u == 5:
                        pre(i + 1, 1 - b)
                    if more and u == 9:
                        route(i + 1)

            pre(0, 0)
            route(0)
            run_groups(act, experts)

        @block.vector
        def _(dve):
            V = nc.vector

            def A2(i, n):
                k, b = kind_of(n), n % 2
                dve.wait_ge(qkv_done, level(qkv_done, i, n))
                if k == SELF:
                    V.tensor_tensor(T3[:, :, :, :], thrice(bA[:, P:P + 160]), thrice(b_self[:, 0:160]), ALU.add)
                    t = V.tensor_tensor(VG[n % 3][:, :, 0:HD], v3(bA[:, P + 160:P + 192], HD), v3(b_self[:, 160:192], HD), ALU.add)
                    t.then_inc(tok, 1)
                elif k == CROSS:
                    V.tensor_tensor(T[:, :], bA[:, P:3 * P], b_cross[:, 0:2 * P], ALU.add)
                    t = V.tensor_tensor(VC[n % 3][:, :, 0:HD], v3(bA[:, 3 * P:4 * P], HD), v3(b_cross[:, 2 * P:3 * P], HD), ALU.add)
                    t.then_inc(tok, 1)
                else:
                    src = v3(bA[:, P:P + 160], HD)
                    h = HD // 2
                    V.tensor_tensor(rope1[:, :, :], src, rep(cos_t, 20), ALU.mult).then_inc(tok, 1)
                    V.tensor_tensor(rope2[:, :, 0:h], src[:, :, h:HD], rep(sin_t[:, 0:h], 20), ALU.mult).then_inc(tok, 1)
                    t = V.tensor_tensor(rope2[:, :, h:HD], src[:, :, 0:h], rep(sin_t[:, h:HD], 20), ALU.mult)
                    V.tensor_copy(VG[n % 3][:, :, 0:HD], v3(bA[:, P + 160:P + 192], HD))
                    t.then_inc(tok, 1)
                    dve.wait_ge(tok, level(tok, i, n, 3))
                    V.tensor_tensor(T3[:, :, :, :], thrice(rope1[:, :, :].rearrange("p a b -> p (a b)")),
                                        thrice(rope2[:, :, :].rearrange("p a b -> p (a b)")), ALU.add).then_inc(tok, 1)

            def A3(i, n):
                k, b = kind_of(n), n % 2
                dve.wait_ge(hi_done, level(hi_done, i, n))
                if k == CROSS:
                    if kind_of(n - 1) == CROSS:
                        dve.wait_ge(kz_pool, level(kz_pool, i, n - 1))
                    V.tensor_tensor(c_lo[:, 0, :], bQ[:, 0:P], c_hi[:, 0, :].bitcast(F32), ALU.subtract)
                    t = V.tensor_tensor(c_lo[:, 1, :], bA[:, 0:P], c_hi[:, 1, :].bitcast(F32), ALU.subtract)
                    t.then_inc(lo_done, 1)
                    V.tensor_tensor(Qhi[b][:, :, :], rep(c_hi[:, 0, :].bitcast(F32), 4), last(same_c, P), ALU.mult)
                    t = V.tensor_tensor(Khi[b][:, :, :], rep(c_hi[:, 1, :].bitcast(F32), 4), last(same_r, P), ALU.mult)
                    t.then_inc(kz_done, 1)
                else:
                    V.tensor_tensor(Qs[b][32:64, :], bQ[32:64, :], Qs[b][32:64, :].bitcast(F32), ALU.subtract)
                    t = V.tensor_tensor(K1[64:96, :], bA[64:96, 0:P], K1[64:96, :].bitcast(F32), ALU.subtract)
                    t.then_inc(lo_done, 1)
                    dve.wait_ge(lo_done, level(lo_done, i, n))
                    t = V.tensor_tensor(Kz[b][0:96, :, :], rep(K1[0:96, :].bitcast(F32), 4), last(same_c[0:96, :], P), ALU.mult)
                    t.then_inc(kz_done, 1)

            def A4(i, n, gs):
                k = kind_of(n)
                for g in gs:
                    dve.wait_ge(s_done, level(s_done, i, n, g + 1))
                    dst = negmax[:, g, :] if k != CROSS else negmax[:, :, g]
                    V.tensor_reduce(dst, v3(bS[g % 2][:, :], P), AX.X, ALU.max, negate=True).then_inc(s_max, 1)

            def M(i, n):
                k = kind_of(n)
                dve.wait_ge(s_max, level(s_max, i, n))
                src = negmax[:, :, :]
                if k == CROSS:
                    flat = src.rearrange("p a b -> p (a b)")
                    hi, lo = MxC[:, :, 0], MxC[:, :, 1]
                else:
                    flat = src
                    mv = MxG[:, :, 96:128].rearrange("p g (c d) -> p g c d", d=HD)
                    hi, lo = mv[:, :, :, 0], mv[:, :, :, 1]
                V.tensor_copy(hi.bitcast(F32R), flat).then_inc(m_hi, 1)
                dve.wait_ge(m_hi, level(m_hi, i, n))
                V.tensor_tensor(lo, flat, hi, ALU.subtract).then_inc(m_done, 1)

            def A5(i, n):
                if kind_of(n) == CROSS:
                    dve.wait_ge(mT_done, level(mT_done, i, n))
                    V.tensor_tensor(Mbd[n % 2][:, :, :], rep(bQ[:, 0:P], 4), last(same_c, P), ALU.mult).then_inc(m_evac, 1)

            def C1(i, n):
                k = kind_of(n)
                dve.wait_ge(on_done, level(on_done, i, n))
                ov = bC[:, :].rearrange("p (g c d) -> p g c d", c=4, d=SLOT)
                V.reciprocal(rec[:, :, :], ov[:, :, :, HD]).then_inc(c_dve, 1)
                dve.wait_ge(c_dve, level(c_dve, i, n, 1))
                dst = On[:, :].rearrange("p (g c d) -> p g c d", c=4, d=HD)
                r4 = rec[:, :, :].unsqueeze(3).to_broadcast([P, 4, 4, HD])
                t = V.tensor_tensor(dst, ov[:, :, :, 0:HD], r4, ALU.mult)
                if k != SELF:
                    t.then_inc(o_ready, 1)
                    return
                t.then_inc(c_dve, 1)
                dve.wait_ge(c_dve, level(c_dve, i, n, 2))
                V.bn_stats(st_in[:, :], On[:, :]).then_inc(c_dve, 1)
                dve.wait_ge(c_dve, level(c_dve, i, n, 3))
                dve.sem_inc(waits_carried, 1)
                V.bn_aggr(mv_in[:, :], st_in[:, :]).then_inc(c_dve, 1)

            def C1b(i, n):
                if kind_of(n) == SELF:
                    dve.wait_ge(ln_in, level(ln_in, i, n))
                    V.tensor_scalar(On2[:, :], On[:, :], mv_in[:, 0:1], rs_in[:, 1:2], ALU.subtract, ALU.mult).then_inc(o_ready, 1)

            def C3(i, n):
                k, j = kind_of(n), n % STREAMS
                dve.wait_ge(y_done, level(y_done, i, n))
                if k == ROPE:
                    t = V.tensor_tensor(X3[:, bass.ds(((i + n // STEPS) * STREAMS + j) * P, P)], bC[:, P:2 * P], XS[j][:, :], ALU.add)
                    t.then_inc(res, 1)
                    return
                dve.wait_ge(xb_done, level(xb_done, i, n))
                V.tensor_tensor(R[:, :], bC[:, P:2 * P], XB[j][:, :], ALU.add).then_inc(res, 1)
                dve.wait_ge(res, level(res, i, n))
                V.bn_stats(st_post[:, :], R[:, :]).then_inc(post, 1)
                dve.wait_ge(post, level(post, i, n, 1))
                dve.sem_inc(waits_carried, 1)
                V.bn_aggr(mv_post[:, :], st_post[:, :]).then_inc(post, 1)

            def D(i, n):
                k, j = kind_of(n), n % STREAMS
                if k == ROPE:
                    return
                dve.wait_ge(ln_post, level(ln_post, i, n, 2))
                V.tensor_scalar(XS[j][:, :], R[:, :], mv_post[:, 0:1], rs_post[:, 1:2], ALU.subtract, ALU.mult).then_inc(xs_done, 1)
                dve.wait_ge(xs_done, level(xs_done, i, n))
                dve.wait_ge(ln_post, level(ln_post, i, n))
                V.tensor_scalar(H[j][:, :], XS[j][:, :], rs_post[:, 5:6], None, ALU.mult).then_inc(h_done, 1)

            def slot(i, n):
                a, b, c, d = exists(i, n), exists(i, n - 1), exists(i, n - 2), exists(i, n - 3)
                if b:
                    A4(i, n - 1, [2])
                if a:
                    A2(i, n)
                if b:
                    A4(i, n - 1, [3])
                    M(i, n - 1)
                if a:
                    A3(i, n)
                if d:
                    D(i, n - 3)
                if b:
                    A5(i, n - 1)
                if c:
                    C1(i, n - 2)
                if a:
                    A4(i, n, [0, 1])
                if c:
                    C1b(i, n - 2)
                    C3(i, n - 2)

            dve.wait_ge(w_ld, W_ALL)
            dve.wait_ge(init_pool, INIT_POOL)
            V.tensor_copy(ident_b[:, :], ident[:, :])
            V.tensor_copy(mask_b[:, :, :], rep(mask_f[:, :], 4))
            for b in range(2):
                V.tensor_tensor(Kz[b][96:128, :, :], rep(ones_f[96:128, :], 4), last(slot3_one[96:128, :], P), ALU.mult)
            V.tensor_tensor(ones_r[:, :, :], rep(ones_f[:, :], 4), last(cross_one, P), ALU.mult)
            V.tensor_copy(gate_r[:, 0, :], gate_f[:, :]).then_inc(init_dve, 1)
            dve.wait_ge(init_dve, 1)
            V.tensor_tensor(gate_r[:, 1, :], gate_f[:, :], gate_r[:, 0, :].bitcast(F32), ALU.subtract)
            run_slots(dve, slot)

            half = E * F
            for q in range(2):
                dve.wait_ge(init_act, q + 1)
                V.tensor_tensor(w13_lo[:, half * q:half * q + half], w13_f[:, half * q:half * q + half],
                                w13_hi[:, half * q:half * q + half].bitcast(F32), ALU.subtract).then_inc(w13_split, 1)

            def x3(i, t4):
                return X3[:, bass.ds((i * STREAMS + t4) * P, P)]

            def pre(i, b):
                for t4 in range(4):
                    V.bn_stats(st4[:, t4, :], x3(i, t4)).then_inc(pre_st, 1)
                for t4 in range(4):
                    dve.wait_ge(pre_st, level2(pre_st, i, t4 + 1))
                    dve.sem_inc(waits_carried, 1)
                    t = V.bn_aggr(mv4[:, t4, :], st4[:, t4, :])
                t.then_inc(pre_st, 1)
                dve.wait_ge(pre_st, level2(pre_st, i, 5))
                V.tensor_tensor(q4[:, :, 0:1], mv4[:, :, 0:1], mv4[:, :, 0:1], ALU.mult).then_inc(pre_q, 1)
                dve.wait_ge(pre_rs, level2(pre_rs, i, 1))
                for t4 in range(4):
                    V.tensor_scalar(H2[:, t4, :], x3(i, t4), rs4[:, t4, :], None, ALU.mult).then_inc(pre_h, 1)

            def pre2(i, b):
                dve.wait_ge(pre_hi, level2(pre_hi, i, 1))
                V.scalar_tensor_tensor(hT_lo[b][:, :], bQ[:, :], norm_2, hT_hi[b][:, :].bitcast(F32), ALU.mult,
                                       ALU.subtract).then_inc(pre_lo, 1)

            def route1(i):
                dve.wait_ge(pre_g, level2(pre_g, i, 1))
                V.tensor_copy(lg[:, :, :], v3(bC[:, 0:4 * E], E)).then_inc(rt, 1)
                dve.wait_ge(rt, level2(rt, i, 1))
                dve.sem_inc(waits_carried, 1)
                for t4 in range(4):
                    V.max(top8[:, t4, :], lg[:, t4, :]).then_inc(rt, 1)
                for t4 in range(4):
                    dve.wait_ge(rt, level2(rt, i, 2 + t4))
                    dve.sem_inc(waits_carried, 1)
                    V.max_index(idx8[:, t4, :], top8[:, t4, :], lg[:, t4, :]).then_inc(rt, 1)
                V.tensor_tensor(lg2[:, :, :], lg[:, :, :], top8[:, :, 0:1].to_broadcast([P, 4, E]), ALU.subtract
                                ).then_inc(rt, 1)

            def route2(i, b):
                dve.wait_ge(rt, level2(rt, i, 9))
                V.tensor_copy(idxf[:, :, :], idx8[:, :, :]).then_inc(rt, 1)
                dve.wait_ge(rt, level2(rt, i, 11))
                io = rep(iota_e, 4)
                V.tensor_tensor(hot[:, :, :], io, idxf[:, :, 0:1].to_broadcast([P, 4, E]), ALU.is_equal).then_inc(rt, 1)
                V.tensor_tensor(hot2[:, :, :], io, idxf[:, :, 1:2].to_broadcast([P, 4, E]), ALU.is_equal).then_inc(rt, 1)
                dve.wait_ge(rt, level2(rt, i, 13))
                V.tensor_tensor(hot[:, :, :], hot[:, :, :], hot2[:, :, :], ALU.add).then_inc(rt, 1)
                dve.wait_ge(rt_exp, level2(rt_exp, i, 1))
                dve.wait_ge(rt, level2(rt, i, 14))
                V.tensor_tensor(hot2[:, :, :], hot[:, :, :], ex[:, :, :], ALU.mult).then_inc(rt, 1)
                dve.wait_ge(rt, level2(rt, i, 15))
                V.tensor_reduce(wsum[:, :, 0], hot2[:, :, :], AX.X, ALU.add).then_inc(rt, 1)
                dve.wait_ge(rt, level2(rt, i, 16))
                V.reciprocal(wrec[:, :, :], wsum[:, :, :]).then_inc(rt, 1)
                dve.wait_ge(rt, level2(rt, i, 17))
                V.scalar_tensor_tensor(Wr[b][:, :, :], hot2[:, :, :], 0.5, wrec[:, :, :].to_broadcast([P, 4, E]),
                                       ALU.mult, ALU.mult).then_inc(wr_done, 1)

            def weigh(i, b, e):
                dve.wait_ge(y2_done, level2(y2_done, i, e + 1))
                if past(i, e - 2):
                    dve.wait_ge(acc_done, level2(acc_done, i, e - 1))
                y = (bA, bO)[e % 2]
                V.tensor_tensor(yw[e % 2][:, :, :], v3(y[:, :], P), Wr[b][:, :, e:e + 1].to_broadcast([P, 4, P]),
                                ALU.mult).then_inc(yw_done, 1)

            def final1(i, b):
                dve.wait_ge(acc_done, level2(acc_done, i, E))
                for t4 in range(4):
                    V.bn_stats(st_f[:, t4, :], acc[b][:, t4, :]).then_inc(fin_st, 1)
                for t4 in range(4):
                    dve.wait_ge(fin_st, level2(fin_st, i, t4 + 1))
                    dve.sem_inc(waits_carried, 1)
                    t = V.bn_aggr(mv_f[:, t4, :], st_f[:, t4, :])
                t.then_inc(fin_st, 1)

            def final2(i, b):
                dve.wait_ge(fin_rs, level2(fin_rs, i, 2))
                if not (isinstance(i, int) and i < 2):
                    dve.wait_ge(out_done[b], 8 * (i - b))
                for t4 in range(4):
                    V.tensor_scalar(fin[b][:, t4, :], acc[b][:, t4, :], mv_f[:, t4, 0:1], rs_f[:, t4, 1:2], ALU.subtract,
                                    ALU.mult).then_inc(fin_done, 1)

            def experts(i, b, more):
                first = isinstance(i, int) and i == 0
                for u in range(n_units):
                    dve.wait_ge(tanh_done, level2(tanh_done, i, u + 1))
                    V.scalar_tensor_tensor(sg[u % 2][:, :], th[u % 2][:, :], 1.0, bS[u % 2][:, :], ALU.add, ALU.mult
                                           ).then_inc(sg_done, 1)
                    dve.wait_ge(sg_done, level2(sg_done, i, u + 1))
                    if past(i, u - 4):
                        dve.wait_ge(y2_done, level2(y2_done, i, (u - 4) // FC + 1))
                    V.tensor_tensor(G[u % 4][:, :], sg[u % 2][:, :], bT[u % 2][:, :], ALU.mult).then_inc(g_done, 1)
                    if u % FC == 0 and u >= 2 * FC:
                        weigh(i, b, u // FC - 2)
                    if more:
                        if u == 3:
                            pre(i + 1, 1 - b)
                        if u == 6:
                            pre2(i + 1, 1 - b)
                        if u == 8:
                            route1(i + 1)
                        if u == 10:
                            route2(i + 1, 1 - b)
                    if not first and u == 1:
                        final1(i - 1, 1 - b)
                    if not first and u == 2:
                        final2(i - 1, 1 - b)
                weigh(i, b, E - 2)
                weigh(i, b, E - 1)

            pre(0, 0)
            pre2(0, 0)
            route1(0)
            route2(0, 0)
            run_groups(dve, experts)
            final1(ITER - 1, 1)
            final2(ITER - 1, 1)

        @block.gpsimd
        def _(pool):
            G_ = nc.gpsimd

            def xb(i, n):
                k, j = kind_of(n), n % STREAMS
                if k == ROPE:
                    return
                if k == SELF:
                    pool.wait_ge(x_ld[j], 16 * (i + 1))
                    if exists(i, n - STREAMS):
                        pool.wait_ge(res, level(res, i, n - STREAMS))
                else:
                    pool.wait_ge(xs_done, level(xs_done, i, n - STREAMS))
                src = XL[j] if k == SELF else XS[j]
                G_.tensor_tensor(XB[j][:, :], src[:, :], b_out[k], ALU.add).then_inc(xb_done, 1)

            def kz(i, n):
                b = n % 2
                if kind_of(n) == CROSS:
                    pool.wait_ge(lo_done, level(lo_done, i, n))
                    G_.tensor_tensor(Qlo[b][:, :, :], rep(c_lo[:, 0, :].bitcast(F32), 4), last(same_c, P), ALU.mult)
                    G_.tensor_tensor(Klo[b][:, :, :], rep(c_lo[:, 1, :].bitcast(F32), 4), last(same_r, P), ALU.mult).then_inc(kz_pool, 1)

            def sel(i, n, cs):
                if kind_of(n) == CROSS:
                    return
                for c in cs:
                    pool.wait_ge(exp_done, level(exp_done, i, n, c + 1))
                    pool.sem_inc(waits_carried, 1)
                    G_.affine_select(out=v3(PT[c][:, :], P), in_=v3(PT[c][:, :], P), pattern=[[0, 4], [1, P]],
                                         compare_op=ALU.is_ge, fill=0.0, base=0, channel_multiplier=-1).then_inc(causal, 1)

            def rs_inner(i, n):
                if kind_of(n) != SELF:
                    return
                pool.wait_ge(c_dve, level(c_dve, i, n))
                G_.tensor_tensor(rs_in[:, 0:1], mv_in[:, 1:2], eps_col, ALU.add).then_inc(ln_in, 1)
                pool.wait_ge(ln_in, level(ln_in, i, n, 1))
                G_.tensor_tensor(rs_in[:, 1:2], rs_in[:, 0:1], minus_half, ALU.pow).then_inc(ln_in, 1)

            def rs_after(i, n):
                if kind_of(n) == ROPE:
                    pool.wait_ge(res, level(res, i, n))
                    col = bass.ds(((i + n // STEPS) * STREAMS + n % STREAMS) * P, P)
                    G_.tensor_tensor(X23[:, col], X3[:, col], XS[n % STREAMS][:, :], ALU.add).then_inc(xb_done, 1)
                    return
                pool.wait_ge(post, level(post, i, n))
                G_.tensor_tensor(rs_post[:, 0:1], mv_post[:, 1:2], eps_col, ALU.add).then_inc(ln_post, 1)
                pool.wait_ge(ln_post, level(ln_post, i, n, 1))
                G_.tensor_tensor(rs_post[:, 1:2], rs_post[:, 0:1], minus_half, ALU.pow).then_inc(ln_post, 1)
                pool.wait_ge(ln_post, level(ln_post, i, n, 2))
                G_.tensor_tensor(rs_post[:, 2:3], rs_post[:, 1:2], mv_post[:, 1:2], ALU.mult).then_inc(ln_post, 1)
                pool.wait_ge(ln_post, level(ln_post, i, n, 3))
                G_.tensor_tensor(rs_post[:, 3:4], rs_post[:, 1:2], rs_post[:, 2:3], ALU.mult).then_inc(ln_post, 1)
                pool.wait_ge(ln_post, level(ln_post, i, n, 4))
                G_.tensor_tensor(rs_post[:, 4:5], rs_post[:, 3:4], eps_col, ALU.add).then_inc(ln_post, 1)
                pool.wait_ge(ln_post, level(ln_post, i, n, 5))
                G_.tensor_tensor(rs_post[:, 5:6], rs_post[:, 4:5], minus_half, ALU.pow).then_inc(ln_post, 1)

            def slot(i, n):
                a, b, c, d = exists(i, n), exists(i, n - 1), exists(i, n - 2), exists(i, n - 3)
                if d:
                    rs_after(i, n - 3)
                if c:
                    sel(i, n - 2, [2, 3])
                if a:
                    xb(i, n)
                    kz(i, n)
                if b:
                    sel(i, n - 1, [0, 1])
                if c:
                    rs_inner(i, n - 2)

            G_.memset(MxG[:, :, :], 0.0)
            G_.memset(MxC[:, :, :], 0.0)
            G_.memset(ones_f[:, :], 1.0)
            for b in range(3):
                G_.memset(VG[b][:, :, :], 0.0)
                G_.memset(VC[b][:, :, :], 0.0)
            pool_set = G_.memset(rs_in[:, :], 0.0)
            pool_set.then_inc(pool_zero, 1)
            pool.wait_ge(pool_zero, 1)
            for b in range(3):
                G_.memset(VG[b][:, :, HD:HD + 1], 1.0)
                t = G_.memset(VC[b][:, :, HD:HD + 1], 1.0)
            t.then_inc(init_pool, 1)
            pool.wait_ge(w_ld, W_ALL)
            run_slots(pool, slot)

            def pre(i):
                pool.wait_ge(pre_q, level2(pre_q, i, 1))
                G_.tensor_tensor(q4[:, :, 1:2], q4[:, :, 0:1], mv4[:, :, 1:2], ALU.add).then_inc(pre_pool, 1)
                pool.wait_ge(pre_pool, level2(pre_pool, i, 1))
                G_.tensor_tensor(q4[:, :, 0:1], q4[:, :, 1:2], rep(eps_col, 4), ALU.add).then_inc(pre_pool, 1)
                pool.wait_ge(pre_pool, level2(pre_pool, i, 2))
                G_.tensor_tensor(rs4[:, :, :], q4[:, :, 0:1], rep(minus_half, 4), ALU.pow).then_inc(pre_rs, 1)

            def accumulate(i, b, e):
                pool.wait_ge(yw_done, level2(yw_done, i, e + 1))
                if e == 0:
                    if not (isinstance(i, int) and i < 2):
                        pool.wait_ge(fin_done, level2(fin_done, i - 2, 4))
                    src = v3(X23[:, bass.ds(i * N, N)], P)
                else:
                    pool.wait_ge(acc_done, level2(acc_done, i, e))
                    src = acc[b][:, :, :]
                G_.tensor_tensor(acc[b][:, :, :], src, yw[e % 2][:, :, :], ALU.add).then_inc(acc_done, 1)

            def final(i):
                pool.wait_ge(fin_st, level2(fin_st, i, 5))
                G_.tensor_tensor(rs_f[:, :, 0:1], mv_f[:, :, 1:2], rep(eps_col, 4), ALU.add).then_inc(fin_rs, 1)
                pool.wait_ge(fin_rs, level2(fin_rs, i, 1))
                G_.tensor_tensor(rs_f[:, :, 1:2], rs_f[:, :, 0:1], rep(minus_half, 4), ALU.pow).then_inc(fin_rs, 1)

            def experts(i, b, more):
                first = isinstance(i, int) and i == 0
                if not first:
                    final(i - 1)
                if more:
                    pre(i + 1)
                for e in range(E):
                    accumulate(i, b, e)

            pre(0)
            pool.wait_ge(xb_done, level(xb_done, ITER, -1))
            run_groups(pool, experts)
            final(ITER - 1)



def kernel(**inputs):
    import numpy as np
    import concourse.bacc as bacc
    from concourse.bass_utils import run_bass_kernel_spmd as run

    a = {k: np.asarray(v) for k, v in inputs.items()}
    C = np.ascontiguousarray
    f = np.float32
    T = 128

    def q_order(w):
        return w.reshape(4, 4, 8, -1).transpose(1, 0, 2, 3).reshape(128, -1)

    wqkv = a["L0_ffn_wqkv"]
    w_rope = np.concatenate([q_order(wqkv[:128]), wqkv[128:]], axis=0).T
    wo_rope = q_order(a["L0_ffn_wo"].T)
    rows = np.concatenate([a[k] for k in ("L0_attn_bq", "L0_attn_bk", "L0_attn_bv", "L0_xattn_b_q", "L0_xattn_b_kv",
                                          "L0_attn_bo", "L0_xattn_b_out")])
    feat = np.stack([a[k] for k in ("L0_attn_ln_g", "L0_attn_ln_b", "L0_xattn_w_norm", "L0_ffn_ln1_w", "L0_ffn_ln2_w")], axis=1)

    p = np.arange(128)
    k4 = np.arange(4)
    same_c = ((p % 32) // 8)[:, None] == k4
    same_r = (p // 32)[:, None] == k4
    inv_freq = f(1.0) / (f(10000.0) ** (np.arange(0, 8, 2, dtype=f) / f(8)))
    ang = np.arange(T, dtype=f)[:, None] * inv_freq[None, :]
    cos, sin = np.cos(ang), np.sin(ang)
    two = (p % 8 < 2)[:, None]
    tables = np.concatenate([same_c, same_r, cos, cos, -sin, sin, same_c & two, same_r & two,
                             np.tile(np.arange(8), (128, 1)), np.full((128, 1), -0.5), np.full((128, 1), EPS)], axis=1).astype(f)
    mask = np.where(p[None, :] > p[:, None], f(NEG), f(0)).astype(f)

    E = a["L0_ffn_gate_w"].shape[0]
    arrays = {
        "x": a["x"],
        "ctx_in": a["ctx_1024"],
        "w_self": np.concatenate([a["L0_attn_Wq"], a["L0_attn_Wk"], a["L0_attn_Wv"]], axis=1),
        "w_crossq": a["L0_xattn_w_q"].T,
        "w_crosskv": a["L0_xattn_w_kv"].T,
        "w_rope": w_rope,
        "w_out": np.stack([a["L0_attn_Wo"], a["L0_xattn_w_out"].T, wo_rope]),
        "bias_rows": np.broadcast_to(rows, (128, rows.size)),
        "feat_cols": feat,
        "tables": tables,
        "ident_in": np.eye(128, dtype=f),
        "mask_in": mask,
        "gate_in": a["L0_ffn_gate_w"].T,
        "w13_in": a["L0_ffn_w13"].transpose(2, 0, 1).reshape(128, -1),
        "w2_in": a["L0_ffn_w2"].reshape(E, 128, -1, 128).transpose(3, 0, 2, 1).reshape(128, -1),
    }
    nc = bacc.Bacc("TRN2", target_bir_lowering=False, num_devices=1)
    arrays = {k: C(v) for k, v in arrays.items()}
    aps = [nc.dram_tensor(k, v.shape, mybir.dt.from_np(v.dtype), kind="ExternalInput").ap() for k, v in arrays.items()]
    out = nc.dram_tensor("out", a["x"].shape, F32, kind="ExternalOutput").ap()
    program(nc, *aps, out)
    r = run(nc, [arrays], core_ids=[0])
    return r.results[0]["out"]
```

```python
from contextlib import ExitStack

import concourse.bass as bass
from concourse import mybir

P = 128
F32 = mybir.dt.float32
F32R = mybir.dt.float32r
BF16 = mybir.dt.bfloat16
U32 = mybir.dt.uint32
ALU = mybir.AluOpType
ACT = mybir.ActivationFunctionType
AX = mybir.AxisListType

HD = 8
SLOT = 32
NEG = -1e30
EPS = 1e-5
SCALE = HD ** -0.5
STREAMS = 4
KINDS = 3
STEPS = STREAMS * KINDS
SELF, CROSS, ROPE = range(KINDS)


def kind_of(n):
    return (n % STEPS) // STREAMS


def program(nc, x, ctx_in, w_self, w_crossq, w_crosskv, w_rope, w_out, bias_rows, feat_cols, tables, ident_in,
            mask_in, gate_in, w13_in, w2_in, out):
    NB = x.shape[0]
    ITER = NB // STREAMS
    E = gate_in.shape[1]
    F = w13_in.shape[1] // (2 * E)
    FC = F // P
    N = STREAMS * P

    with ExitStack() as ctx:
        def sb(name, shape, dt=F32):
            return ctx.enter_context(nc.sbuf_tensor(name, shape, dt))

        def ps(name):
            return ctx.enter_context(nc.psum_tensor(name, [P, 512], F32))

        def sem(name):
            return ctx.enter_context(nc.semaphore(name))

        Wself = sb("Wself", [P, 192])
        Wcq = sb("Wcq", [P, P])
        Wckv = sb("Wckv", [P, 2 * P])
        Wrope = sb("Wrope", [P, 192])
        Wout = sb("Wout", [P, KINDS, P])
        bias = sb("bias", [P, 832])
        b_self, b_cross = bias[:, 0:192], bias[:, 192:576]
        b_out = [bias[:, 576:704], bias[:, 704:832]]
        feat = sb("feat", [P, 5])
        ln_g, ln_b, norm_x, norm_1, norm_2 = [feat[:, k:k + 1] for k in range(5)]
        tab = sb("tab", [P, 4 + 4 + 8 + 8 + 4 + 4 + 8 + 1 + 1])
        same_c, same_r, cos_t, sin_t = tab[:, 0:4], tab[:, 4:8], tab[:, 8:16], tab[:, 16:24]
        slot3_one, cross_one, iota_e, minus_half, eps_col = tab[:, 24:28], tab[:, 28:32], tab[:, 32:40], tab[:, 40:41], tab[:, 41:42]
        ident = sb("ident", [P, P])
        ident_b = sb("ident_b", [P, P], BF16)
        mask_f = sb("mask_f", [P, P])
        mask_b = sb("mask_b", [P, 4, P], BF16)
        ones_r = sb("ones_r", [P, 4, P], F32R)
        ones_f = sb("ones_f", [P, P])
        gate_f = sb("gate_f", [P, E])
        gate_r = sb("gate_r", [P, 2, E], F32R)
        w13_f = sb("w13_f", [P, 2 * E * F])
        w13_hi = sb("w13_hi", [P, 2 * E * F], F32R)
        w13_lo = sb("w13_lo", [P, 2 * E * F], F32R)
        w2_f = sb("w2_f", [P, E * FC * P])

        XL = [sb(f"XL{j}", [P, P]) for j in range(STREAMS)]
        CL = [sb(f"CL{j}", [P, P]) for j in range(STREAMS)]
        XS = [sb(f"XS{j}", [P, P]) for j in range(STREAMS)]
        H = [sb(f"H{j}", [P, P]) for j in range(STREAMS)]
        XB = [sb(f"XB{j}", [P, P]) for j in range(STREAMS)]
        xTs = sb("xTs", [P, P])
        cTs = sb("cTs", [P, P])
        T = sb("T", [P, 2 * P])
        T3 = sb("T3", [P, 5, 3, SLOT])
        rope1 = sb("rope1", [P, 20, HD])
        rope2 = sb("rope2", [P, 20, HD])
        VG = [sb(f"VG{b}", [P, 4, SLOT]) for b in range(3)]
        VC = [sb(f"VC{b}", [P, 16, SLOT]) for b in range(3)]
        Qs = [sb(f"Qs{b}", [P, 512], F32R) for b in range(2)]
        K1 = sb("K1", [P, P], F32R)
        Kz = [sb(f"Kz{b}", [P, 4, P], F32R) for b in range(2)]
        c_hi = sb("c_hi", [P, 2, P], F32R)
        c_lo = sb("c_lo", [P, 2, P], F32R)
        Qhi = [sb(f"Qhi{b}", [P, 4, P], F32R) for b in range(2)]
        Qlo = [sb(f"Qlo{b}", [P, 4, P], F32R) for b in range(2)]
        Khi = [sb(f"Khi{b}", [P, 4, P], F32R) for b in range(2)]
        Klo = [sb(f"Klo{b}", [P, 4, P], F32R) for b in range(2)]
        Mbd = [sb(f"Mbd{b}", [P, 4, P], F32R) for b in range(2)]
        negmax = sb("negmax", [P, 4, 4])
        MxG = sb("MxG", [P, 4, SLOT])
        MxC = sb("MxC", [P, 16, HD])
        PT = [sb(f"PT{c}", [P, 512]) for c in range(4)]
        OTs = sb("OTs", [P, 512])
        rec = sb("rec", [P, 4, 4])
        On = sb("On", [P, P])
        On2 = sb("On2", [P, P])
        OnT = sb("OnT", [P, P])
        R = sb("R", [P, P])
        st_in = sb("st_in", [P, 6])
        mv_in = sb("mv_in", [P, 2])
        rs_in = sb("rs_in", [P, 2])
        st_post = sb("st_post", [P, 6])
        mv_post = sb("mv_post", [P, 2])
        rs_post = sb("rs_post", [P, 6])
        X3 = sb("X3", [P, NB * P])
        X23 = sb("X23", [P, NB * P])

        st4 = sb("st4", [P, 4, 6])
        mv4 = sb("mv4", [P, 4, 2])
        q4 = sb("q4", [P, 4, 2])
        rs4 = sb("rs4", [P, 4, 1])
        H2 = sb("h_moe", [P, 4, P])
        hT_hi = [sb(f"hT_hi{b}", [P, N], F32R) for b in range(2)]
        hT_lo = [sb(f"hT_lo{b}", [P, N], F32R) for b in range(2)]
        lg = sb("lg", [P, 4, E])
        top8 = sb("top8", [P, 4, 8])
        idx8 = sb("idx8", [P, 4, 8], U32)
        idxf = sb("idxf", [P, 4, 8])
        neg_top = sb("neg_top", [P, 4, 1])
        lg2 = sb("lg2", [P, 4, E])
        ex = sb("ex", [P, 4, E])
        hot = sb("hot", [P, 4, E])
        hot2 = sb("hot2", [P, 4, E])
        wsum = sb("wsum", [P, 4, 1])
        wrec = sb("wrec", [P, 4, 1])
        Wr = [sb(f"Wr{b}", [P, 4, E]) for b in range(2)]
        th = [sb(f"th{b}", [P, N]) for b in range(2)]
        sg = [sb(f"sg{b}", [P, N]) for b in range(2)]
        G = PT
        yw = [sb(f"yw{b}", [P, 4, P]) for b in range(2)]
        acc = [sb(f"acc{b}", [P, 4, P]) for b in range(2)]
        st_f = sb("st_f", [P, 4, 6])
        mv_f = sb("mv_f", [P, 4, 2])
        rs_f = sb("rs_f", [P, 4, 2])
        fin = [sb(f"fin{b}", [P, 4, P]) for b in range(2)]

        bA, bQ, bC, bS0, bS1, bT0, bT1, bO = [ps(f"bank{k}") for k in range(8)]
        bS, bT = [bS0, bS1], [bT0, bT1]

        w_ld = sem("w_ld")
        x_ld = [sem(f"x_ld{j}") for j in range(STREAMS)]
        c_ld = [sem(f"c_ld{j}") for j in range(STREAMS)]
        w13_ld = sem("w13_ld")
        init_pool = sem("init_pool")
        init_dve = sem("init_dve")
        w13_high = sem("w13_high")
        waits_carried = sem("waits_carried")

        CHUNK = 512
        CHUNKS = 2 * E * F // CHUNK
        W_ALL = 16 * 11
        per_step = {}

        def step_sem(name, *counts):
            s = sem(name)
            per_step[s] = counts if len(counts) > 1 else counts * KINDS
            return s

        xT_done = step_sem("xT_done", 1)
        xT_evac = step_sem("xT_evac", 1)
        qkv_done = step_sem("qkv_done", 1)
        tok = step_sem("tok", 1, 1, 4)
        qkT_done = step_sem("qkT_done", 1)
        hi_done = step_sem("hi_done", 1)
        lo_done = step_sem("lo_done", 1)
        kz_done = step_sem("kz_done", 1)
        kz_pool = step_sem("kz_pool", 0, 1, 0)
        s_done = step_sem("s_done", 4)
        s_max = step_sem("s_max", 4)
        m_hi = step_sem("m_hi", 1)
        m_done = step_sem("m_done", 1)
        mT_done = step_sem("mT_done", 1)
        m_evac = step_sem("m_evac", 1)
        st_done = step_sem("st_done", 4)
        exp_done = step_sem("exp_done", 4)
        causal = step_sem("causal", 4, 0, 4)
        pv_done = step_sem("pv_done", 1)
        ot_evac = step_sem("ot_evac", 1)
        on_done = step_sem("on_done", 1)
        c_dve = step_sem("c_dve", 4, 1, 1)
        ln_in = step_sem("ln_in", 2, 0, 0)
        o_ready = step_sem("o_ready", 1)
        oT_done = step_sem("oT_done", 1)
        oT_evac = step_sem("oT_evac", 1)
        y_done = step_sem("y_done", 1)
        xb_done = step_sem("xb_done", 1)
        res = step_sem("res", 1)
        post = step_sem("post", 2, 2, 0)
        ln_post = step_sem("ln_post", 4, 4, 0)
        xs_done = step_sem("xs_done", 1, 1, 0)
        h_done = step_sem("h_done", 1, 1, 0)

        def level(s, i, n, m=None):
            counts = per_step[s]
            i, n = i + n // STEPS, n % STEPS
            if m is None:
                m = counts[kind_of(n)]
            return i * STREAMS * sum(counts) + sum(counts[kind_of(a)] for a in range(n)) + m

        def exists(i, n):
            if not isinstance(i, int):
                return True
            return 0 <= i * STEPS + n < ITER * STEPS

        def v3(ap, b):
            return ap.rearrange("p (a b) -> p a b", b=b)

        def rep(ap, k):
            return ap.unsqueeze(1).to_broadcast([ap.shape[0], k, ap.shape[1]])

        def last(ap, k):
            return ap.unsqueeze(2).to_broadcast([ap.shape[0], ap.shape[1], k])

        def thrice(ap):
            return v3(ap, SLOT).unsqueeze(2).to_broadcast([P, 5, 3, SLOT])

        block = ctx.enter_context(nc.Block())

        per_group = {}

        def p2(name, per_iter):
            s = sem(name)
            per_group[s] = per_iter
            return s

        w13_split = sem("w13_split")
        n_units = E * FC
        pre_st = p2("pre_st", 5)
        pre_q = p2("pre_q", 1)
        pre_rs = p2("pre_rs", 1)
        pre_h = p2("pre_h", 4)
        pre_t = p2("pre_t", 1)
        pre_hi = p2("pre_hi", 1)
        pre_lo = p2("pre_lo", 1)
        pre_g = p2("pre_g", 1)
        rt = p2("rt", 17)
        rt_exp = p2("rt_exp", 1)
        xu_done = p2("xu_done", n_units)
        tanh_done = p2("tanh_done", n_units)
        sg_done = p2("sg_done", n_units)
        g_done = p2("g_done", n_units)
        y2_done = p2("y2_done", E)
        yw_done = p2("yw_done", E)
        acc_done = p2("acc_done", E)
        fin_st = p2("fin_st", 5)
        fin_rs = p2("fin_rs", 2)
        fin_done = p2("fin_done", 4)
        wr_done = p2("wr_done", 1)
        pre_pool = p2("pre_pool", 2)
        pool_zero = sem("pool_zero")
        out_done = [sem(f"out_done{b}") for b in range(2)]

        def level2(s, i, m):
            return i * per_group[s] + m

        def past(i, k):
            return not isinstance(i, int) or i > 0 or k >= 0

        @block.sync
        def _(sp):
            def load(i, which):
                for j in range(STREAMS):
                    b = i * STREAMS + j
                    if which == "x":
                        if not (isinstance(i, int) and i == 0):
                            sp.wait_ge(xT_done, level(xT_done, i - 1, j))
                            sp.sem_inc(waits_carried, 1)
                            sp.wait_ge(xb_done, level(xb_done, i - 1, j))
                            sp.sem_inc(waits_carried, 1)
                        sp.dma_start(XL[j][:, :], x[bass.ds(b, 1), :, :].rearrange("b s d -> (b s) d")
                                     ).then_inc(x_ld[j], 16)
                    else:
                        if not (isinstance(i, int) and i == 0):
                            sp.wait_ge(xT_done, level(xT_done, i - 1, STREAMS + j))
                            sp.sem_inc(waits_carried, 1)
                        sp.dma_start(CL[j][:, :], ctx_in[bass.ds(b, 1), :, :].rearrange("b s d -> (b s) d")
                                     ).then_inc(c_ld[j], 16)

            sp.dma_start(ident[:, :], ident_in).then_inc(w_ld, 16)
            sp.dma_start(XL[0][:, :], x[0, :, :]).then_inc(x_ld[0], 16)
            sp.dma_start(Wself[:, :], w_self).then_inc(w_ld, 16)
            sp.dma_start(tab[:, :], tables).then_inc(w_ld, 16)
            sp.dma_start(bias[:, :], bias_rows).then_inc(w_ld, 16)
            sp.dma_start(mask_f[:, :], mask_in).then_inc(w_ld, 16)
            sp.dma_start(feat[:, :], feat_cols).then_inc(w_ld, 16)
            sp.dma_start(Wout[:, :, :], w_out.rearrange("k p n -> p k n")).then_inc(w_ld, 16)
            sp.dma_start(Wcq[:, :], w_crossq).then_inc(w_ld, 16)
            sp.dma_start(Wckv[:, :], w_crosskv).then_inc(w_ld, 16)
            sp.dma_start(Wrope[:, :], w_rope).then_inc(w_ld, 16)
            sp.dma_start(gate_f[:, :], gate_in).then_inc(w_ld, 16)
            for j in range(1, STREAMS):
                sp.dma_start(XL[j][:, :], x[j, :, :]).then_inc(x_ld[j], 16)
            load(0, "c")
            sp.dma_start(w13_f[:, :], w13_in).then_inc(w13_ld, 16)
            sp.dma_start(w2_f[:, :], w2_in).then_inc(w13_ld, 16)
            with sp.Fori(1, ITER) as i:
                load(i, "x")
                load(i, "c")

            def store(i, b):
                sp.wait_ge(fin_done, level2(fin_done, i, 4))
                sp.sem_inc(waits_carried, 1)
                sp.dma_start(out[bass.ds(i * STREAMS, STREAMS), :, :].rearrange("b s d -> s b d"),
                             fin[b][:, :, :]).then_inc(out_done[b], 16)

            with sp.Fori(0, ITER // 2) as h:
                for b in range(2):
                    store(h * 2 + b, b)
            for b in range(2):
                sp.wait_ge(out_done[b], 16 * (ITER // 2))


        def run_slots(eng, slot, split_w13=None):
            for n in range(STEPS):
                slot(0, n)
                if split_w13 and n >= STEPS - CHUNKS:
                    split_w13(n - (STEPS - CHUNKS))
            with eng.Fori(1, ITER) as i:
                for n in range(STEPS):
                    slot(i, n)
            for n in range(4):
                slot(ITER, n)

        def run_groups(eng, body):
            body(0, 0, True)
            body(1, 1, True)
            with eng.Fori(1, ITER // 2 - 1) as h:
                body(h * 2, 0, True)
                body(h * 2 + 1, 1, True)
            body(ITER - 2, 0, True)
            body(ITER - 1, 1, False)

        INIT_POOL = 1
        INIT_DVE = 1


        @block.tensor
        def _(pe):
            mm = nc.tensor.matmul

            def A1(i, n):
                k, j = kind_of(n), n % STREAMS
                if k == SELF:
                    pe.wait_ge(x_ld[j], 16 * (i + 1))
                else:
                    pe.wait_ge(h_done, level(h_done, i, n - STREAMS))
                if exists(i, n - 1):
                    pe.wait_ge(lo_done, level(lo_done, i, n - 1))
                src = XL[j] if k == SELF else H[j]
                t = nc.tensor.transpose(bA[:, 0:P], src[:, :], ident[:, :])
                if k == CROSS:
                    pe.wait_ge(c_ld[j], 16 * (i + 1))
                    t = nc.tensor.transpose(bA[:, 2 * P:3 * P], CL[j][:, :], ident[:, :])
                t.then_inc(xT_done, 1)

            def A2(i, n):
                k = kind_of(n)
                pe.wait_ge(xT_evac, level(xT_evac, i, n))
                if k == CROSS:
                    mm(bA[:, P:2 * P], xTs[:, :], Wcq[:, :], start=True, stop=True)
                    t = mm(bA[:, 2 * P:4 * P], cTs[:, :], Wckv[:, :], start=True, stop=True)
                else:
                    t = mm(bA[:, P:P + 192], xTs[:, :], (Wself if k == SELF else Wrope)[:, :], start=True, stop=True)
                t.then_inc(qkv_done, 1)

            def A3(i, n):
                k = kind_of(n)
                pe.wait_ge(tok, level(tok, i, n))
                if k == CROSS:
                    nc.tensor.transpose(bQ[:, 0:P], T[:, 0:P], ident[:, :])
                    t = nc.tensor.transpose(bA[:, 0:P], T[:, P:2 * P], ident[:, :])
                else:
                    for g in range(4):
                        nc.tensor.transpose(bQ[0:96, P * g:P * g + P], T3[:, g, :, :], ident[:, :])
                    t = nc.tensor.transpose(bA[0:96, 0:P], T3[:, 4, :, :], ident[:, :])
                t.then_inc(qkT_done, 1)

            def A4(i, n, gs):
                k, b = kind_of(n), n % 2
                if 0 in gs:
                    pe.wait_ge(kz_done, level(kz_done, i, n))
                for g in gs:
                    if exists(i, n - 1) or g >= 2:
                        pe.wait_ge(s_max, level(s_max, i, n, g - 1))
                    if k == CROSS:
                        t = mm(bS[g % 2][:, :], Qhi[b][:, g, :], Khi[b][:, :, :], start=True, stop=True)
                    else:
                        mm(bS[g % 2][:, :], Qs[b][0:96, P * g:P * g + P], Kz[b][0:96, :, :], start=True, stop=False)
                        t = mm(bS[g % 2][:, :], ident_b[:, :], mask_b[:, :, :], start=False, stop=True)
                    t.then_inc(s_done, 1)

            def A5(i, n):
                k = kind_of(n)
                pe.wait_ge(m_done, level(m_done, i, n))
                if exists(i, n - 1):
                    pe.wait_ge(ot_evac, level(ot_evac, i, n - 1))
                if k == CROSS:
                    t = nc.tensor.transpose(bO[:, 0:P], MxC[:, :, :], ident[:, :])
                else:
                    t = nc.tensor.transpose(bO[:, 0:P], MxG[:, :, :], ident[:, :])
                t.then_inc(mT_done, 1)

            def B1(i, n, cs):
                k, b = kind_of(n), n % 2
                if 0 in cs:
                    pe.wait_ge(m_evac, level(m_evac, i, n))
                    if k == CROSS:
                        pe.wait_ge(kz_pool, level(kz_pool, i, n))
                for c in cs:
                    if exists(i, n - 1) or c >= 2:
                        pe.wait_ge(exp_done, level(exp_done, i, n, c - 1))
                    o = bT[c % 2][:, :]
                    if k == CROSS:
                        mm(o, Khi[b][:, c, :], Qhi[b][:, :, :], start=True, stop=False)
                        mm(o, Khi[b][:, c, :], Qlo[b][:, :, :], start=False, stop=False)
                        mm(o, Klo[b][:, c, :], Qhi[b][:, :, :], start=False, stop=False)
                        t = mm(o, ones_r[:, c, :], Mbd[b][:, :, :], start=False, stop=True)
                    else:
                        t = mm(o, Kz[b][:, c, :], Qs[b][:, :], start=True, stop=True)
                    t.then_inc(st_done, 1)

            def B2(i, n):
                k, b = kind_of(n), n % 2
                if exists(i, n - 1):
                    pe.wait_ge(ot_evac, level(ot_evac, i, n - 1))
                for c in range(4):
                    if k == CROSS:
                        pe.wait_ge(exp_done, level(exp_done, i, n, c + 1))
                        for h in range(4):
                            t = mm(bO[SLOT * h:SLOT * h + SLOT, P * c:P * c + P], VC[n % 3][:, 4 * c + h, :],
                                   PT[c][:, P * h:P * h + P], start=True, stop=True, tile_position=(0, SLOT * h))
                    else:
                        pe.wait_ge(causal, level(causal, i, n, c + 1))
                        t = mm(bO[SLOT * c:SLOT * c + SLOT, :], VG[n % 3][:, c, :], PT[c][:, :], start=True, stop=True,
                               tile_position=(0, SLOT * c))
                t.then_inc(pv_done, 1)

            def C1(i, n):
                pe.wait_ge(ot_evac, level(ot_evac, i, n))
                if exists(i, n - 1):
                    pe.wait_ge(res, level(res, i, n - 1))
                for g in range(4):
                    t = nc.tensor.transpose(v3(bC[:, :], P)[:, g, :], OTs[:, P * g:P * g + P], ident[:, :])
                t.then_inc(on_done, 1)

            def C2(i, n):
                pe.wait_ge(o_ready, level(o_ready, i, n))
                t = nc.tensor.transpose(bC[:, 0:P], (On2 if kind_of(n) == SELF else On)[:, :], ident[:, :])
                t.then_inc(oT_done, 1)

            def C3(i, n):
                pe.wait_ge(oT_evac, level(oT_evac, i, n))
                mm(bC[:, P:2 * P], OnT[:, :], Wout[:, kind_of(n), :], start=True, stop=True).then_inc(y_done, 1)

            def slot(i, n):
                if exists(i, n - 3):
                    B1(i, n - 3, [1])
                if exists(i, n - 1):
                    A2(i, n - 1)
                if exists(i, n - 2):
                    A4(i, n - 2, [2])
                if exists(i, n - 3):
                    B1(i, n - 3, [2])
                if exists(i, n - 2):
                    A4(i, n - 2, [3])
                if exists(i, n - 4):
                    C2(i, n - 4)
                if exists(i, n - 3):
                    B1(i, n - 3, [3])
                if exists(i, n - 1):
                    A3(i, n - 1)
                if exists(i, n - 4):
                    C3(i, n - 4)
                if exists(i, n - 3):
                    B2(i, n - 3)
                if exists(i, n - 2):
                    A5(i, n - 2)
                if exists(i, n - 3):
                    C1(i, n - 3)
                if exists(i, n - 1):
                    A4(i, n - 1, [0])
                if exists(i, n):
                    A1(i, n)
                if exists(i, n - 1):
                    A4(i, n - 1, [1])
                if exists(i, n - 2):
                    B1(i, n - 2, [0])

            pe.wait_ge(w_ld, W_ALL)
            pe.wait_ge(init_pool, INIT_POOL)
            pe.wait_ge(init_dve, INIT_DVE)
            run_slots(pe, slot)

            def pre(i):
                pe.wait_ge(pre_h, level2(pre_h, i, 4))
                for t4 in range(4):
                    t = nc.tensor.transpose(v3(bQ[:, :], P)[:, t4, :], H2[:, t4, :], ident[:, :])
                t.then_inc(pre_t, 1)

            def router(i, b):
                pe.wait_ge(pre_lo, level2(pre_lo, i, 1))
                for t4 in range(4):
                    o = bC[:, E * t4:E * t4 + E]
                    lh, ll = hT_hi[b][:, P * t4:P * t4 + P], hT_lo[b][:, P * t4:P * t4 + P]
                    mm(o, lh, gate_r[:, 0, :], start=True, stop=False)
                    mm(o, lh, gate_r[:, 1, :], start=False, stop=False)
                    t = mm(o, ll, gate_r[:, 0, :], start=False, stop=True)
                t.then_inc(pre_g, 1)

            def unit(i, b, u):
                e, f = u // FC, u % FC
                for w in range(2):
                    o = (bS if w == 0 else bT)[u % 2][:, :]
                    if w == 0:
                        if past(i, u - 2):
                            pe.wait_ge(g_done, level2(g_done, i, u - 1))
                    col = (2 * e + w) * F + f * P
                    mm(o, w13_hi[:, col:col + P], hT_hi[b][:, :], start=True, stop=False)
                    mm(o, w13_hi[:, col:col + P], hT_lo[b][:, :], start=False, stop=False)
                    t = mm(o, w13_lo[:, col:col + P], hT_hi[b][:, :], start=False, stop=True)
                t.then_inc(xu_done, 1)

            def down(i, e):
                y = (bA, bO)[e % 2]
                pe.wait_ge(g_done, level2(g_done, i, FC * (e + 1)))
                if past(i, e - 2):
                    pe.wait_ge(yw_done, level2(yw_done, i, e - 1))
                for t4 in range(4):
                    for f in range(FC):
                        t = mm(y[:, P * t4:P * t4 + P], G[(FC * e + f) % 4][:, P * t4:P * t4 + P],
                               w2_f[:, (e % E * FC + f) * P:(e % E * FC + f + 1) * P], start=(f == 0), stop=(f == FC - 1))
                t.then_inc(y2_done, 1)

            def experts(i, b, more):
                first = isinstance(i, int) and i == 0
                for u in range(n_units):
                    unit(i, b, u)
                    e = u // FC - 1
                    if u % FC == FC - 1 and (e >= 0 or not first):
                        down(i, e)
                    if more and u == 7:
                        pre(i + 1)
                    if more and u == 9:
                        router(i + 1, 1 - b)
                if not more:
                    down(i, E - 1)

            pe.wait_ge(w13_ld, 32)
            pe.wait_ge(w13_split, CHUNKS)
            pre(0)
            router(0, 0)
            run_groups(pe, experts)

        @block.scalar
        def _(act):
            def cp(out_, in_, **kw):
                return nc.scalar.activation(out_, in_, ACT.Identity if kw else ACT.Copy, **kw)

            def A1(i, n):
                k = kind_of(n)
                act.wait_ge(xT_done, level(xT_done, i, n))
                if k == SELF:
                    t = cp(xTs[:, :], bA[:, 0:P])
                elif k == CROSS:
                    cp(xTs[:, :], bA[:, 0:P], scale=norm_x)
                    t = cp(cTs[:, :], bA[:, 2 * P:3 * P])
                else:
                    t = cp(xTs[:, :], bA[:, 0:P], scale=norm_1)
                t.then_inc(xT_evac, 1)

            def A3(i, n):
                k, b = kind_of(n), n % 2
                act.wait_ge(qkT_done, level(qkT_done, i, n))
                if k == CROSS:
                    cp(c_hi[:, 0, :], bQ[:, 0:P])
                    t = cp(c_hi[:, 1, :], bA[:, 0:P])
                else:
                    cp(Qs[b][0:96, :], bQ[0:96, :])
                    t = cp(K1[0:96, :], bA[0:96, 0:P])
                t.then_inc(hi_done, 1)

            def A5(i, n):
                if kind_of(n) != CROSS:
                    act.wait_ge(mT_done, level(mT_done, i, n))
                    for g in range(4):
                        t = cp(Qs[n % 2][96:128, P * g:P * g + P], bO[SLOT * g:SLOT * g + SLOT, 0:P])
                    t.then_inc(m_evac, 1)

            def B1(i, n, cs):
                for c in cs:
                    act.wait_ge(st_done, level(st_done, i, n, c + 1))
                    nc.scalar.activation(PT[c][:, :], bT[c % 2][:, :], ACT.Exp, scale=SCALE).then_inc(exp_done, 1)

            def B2(i, n):
                act.wait_ge(pv_done, level(pv_done, i, n))
                cp(OTs[:, :], bO[:, :]).then_inc(ot_evac, 1)

            def C2(i, n):
                act.wait_ge(oT_done, level(oT_done, i, n))
                kw = dict(scale=ln_g, bias=ln_b) if kind_of(n) == SELF else {}
                cp(OnT[:, :], bC[:, 0:P], **kw).then_inc(oT_evac, 1)

            def slot(i, n):
                if exists(i, n - 1):
                    A3(i, n - 1)
                if exists(i, n - 3):
                    B2(i, n - 3)
                if exists(i, n - 2):
                    A5(i, n - 2)
                if exists(i, n):
                    A1(i, n)
                if exists(i, n - 2):
                    B1(i, n - 2, [0, 1, 2])
                if exists(i, n - 3):
                    C2(i, n - 3)
                if exists(i, n - 2):
                    B1(i, n - 2, [3])

            def split_w13(c):
                col = slice(CHUNK * c, CHUNK * c + CHUNK)
                act.wait_ge(w13_ld, 32)
                cp(w13_hi[:, col], w13_f[:, col]).then_inc(w13_high, 1)

            act.wait_ge(w_ld, W_ALL)
            run_slots(act, slot, split_w13)

            def pre(i, b):
                act.wait_ge(pre_t, level2(pre_t, i, 1))
                cp(hT_hi[b][:, :], bQ[:, :], scale=norm_2).then_inc(pre_hi, 1)

            def route(i):
                act.wait_ge(rt, level2(rt, i, 10))
                nc.scalar.activation(ex[:, :, :], lg2[:, :, :], ACT.Exp).then_inc(rt_exp, 1)

            def experts(i, b, more):
                for u in range(n_units):
                    act.wait_ge(xu_done, level2(xu_done, i, u + 1))
                    if past(i, u - 2):
                        act.wait_ge(sg_done, level2(sg_done, i, u - 1))
                    nc.scalar.activation(th[u % 2][:, :], bS[u % 2][:, :], ACT.Tanh, scale=0.5).then_inc(tanh_done, 1)
                    if more and u == 7:
                        pre(i + 1, 1 - b)
                    if more and u == 11:
                        route(i + 1)

            pre(0, 0)
            route(0)
            run_groups(act, experts)

        @block.vector
        def _(dve):
            V = nc.vector

            def A2(i, n):
                k, b = kind_of(n), n % 2
                dve.wait_ge(qkv_done, level(qkv_done, i, n))
                if k == SELF:
                    V.tensor_tensor(T3[:, :, :, :], thrice(bA[:, P:P + 160]), thrice(b_self[:, 0:160]), ALU.add)
                    t = V.tensor_tensor(VG[n % 3][:, :, 0:HD], v3(bA[:, P + 160:P + 192], HD), v3(b_self[:, 160:192], HD), ALU.add)
                    t.then_inc(tok, 1)
                elif k == CROSS:
                    V.tensor_tensor(T[:, :], bA[:, P:3 * P], b_cross[:, 0:2 * P], ALU.add)
                    t = V.tensor_tensor(VC[n % 3][:, :, 0:HD], v3(bA[:, 3 * P:4 * P], HD), v3(b_cross[:, 2 * P:3 * P], HD), ALU.add)
                    t.then_inc(tok, 1)
                else:
                    src = v3(bA[:, P:P + 160], HD)
                    h = HD // 2
                    V.tensor_tensor(rope1[:, :, :], src, rep(cos_t, 20), ALU.mult).then_inc(tok, 1)
                    V.tensor_tensor(rope2[:, :, 0:h], src[:, :, h:HD], rep(sin_t[:, 0:h], 20), ALU.mult).then_inc(tok, 1)
                    t = V.tensor_tensor(rope2[:, :, h:HD], src[:, :, 0:h], rep(sin_t[:, h:HD], 20), ALU.mult)
                    t.then_inc(tok, 1)

            def A2b(i, n):
                if kind_of(n) == ROPE:
                    V.tensor_copy(VG[n % 3][:, :, 0:HD], v3(bA[:, P + 160:P + 192], HD))
                    dve.wait_ge(tok, level(tok, i, n, 3))
                    V.tensor_tensor(T3[:, :, :, :], thrice(rope1[:, :, :].rearrange("p a b -> p (a b)")),
                                        thrice(rope2[:, :, :].rearrange("p a b -> p (a b)")), ALU.add).then_inc(tok, 1)

            def A3(i, n):
                k, b = kind_of(n), n % 2
                dve.wait_ge(hi_done, level(hi_done, i, n))
                if k == CROSS:
                    if kind_of(n - 1) == CROSS:
                        dve.wait_ge(kz_pool, level(kz_pool, i, n - 1))
                    V.tensor_tensor(c_lo[:, 0, :], bQ[:, 0:P], c_hi[:, 0, :].bitcast(F32), ALU.subtract)
                    t = V.tensor_tensor(c_lo[:, 1, :], bA[:, 0:P], c_hi[:, 1, :].bitcast(F32), ALU.subtract)
                    t.then_inc(lo_done, 1)
                else:
                    V.tensor_tensor(Qs[b][32:64, :], bQ[32:64, :], Qs[b][32:64, :].bitcast(F32), ALU.subtract)
                    t = V.tensor_tensor(K1[64:96, :], bA[64:96, 0:P], K1[64:96, :].bitcast(F32), ALU.subtract)
                    t.then_inc(lo_done, 1)

            def mask_heads(i, n):
                k, b = kind_of(n), n % 2
                if k == CROSS:
                    V.tensor_tensor(Qhi[b][:, :, :], rep(c_hi[:, 0, :].bitcast(F32), 4), last(same_c, P), ALU.mult)
                    t = V.tensor_tensor(Khi[b][:, :, :], rep(c_hi[:, 1, :].bitcast(F32), 4), last(same_r, P), ALU.mult)
                    t.then_inc(kz_done, 1)
                else:
                    dve.wait_ge(lo_done, level(lo_done, i, n))
                    t = V.tensor_tensor(Kz[b][0:96, :, :], rep(K1[0:96, :].bitcast(F32), 4), last(same_c[0:96, :], P), ALU.mult)
                    t.then_inc(kz_done, 1)

            def A4(i, n, gs):
                k = kind_of(n)
                for g in gs:
                    dve.wait_ge(s_done, level(s_done, i, n, g + 1))
                    dst = negmax[:, g, :] if k != CROSS else negmax[:, :, g]
                    V.tensor_reduce(dst, v3(bS[g % 2][:, :], P), AX.X, ALU.max, negate=True).then_inc(s_max, 1)

            def max_parts(n):
                if kind_of(n) == CROSS:
                    return negmax[:, :, :].rearrange("p a b -> p (a b)"), MxC[:, :, 0], MxC[:, :, 1]
                mv = MxG[:, :, :].rearrange("p g (c d) -> p g c d", d=HD)
                return negmax[:, :, :], mv[:, :, :, 0], mv[:, :, :, 1]

            def M1(i, n):
                flat, hi, lo = max_parts(n)
                dve.wait_ge(s_max, level(s_max, i, n))
                V.tensor_copy(hi.bitcast(F32R), flat).then_inc(m_hi, 1)

            def M2(i, n):
                flat, hi, lo = max_parts(n)
                dve.wait_ge(m_hi, level(m_hi, i, n))
                V.tensor_tensor(lo, flat, hi, ALU.subtract).then_inc(m_done, 1)

            def A5(i, n):
                if kind_of(n) == CROSS:
                    dve.wait_ge(mT_done, level(mT_done, i, n))
                    V.tensor_tensor(Mbd[n % 2][:, :, :], rep(bO[:, 0:P], 4), last(same_c, P), ALU.mult).then_inc(m_evac, 1)

            def C1(i, n):
                k = kind_of(n)
                dve.wait_ge(on_done, level(on_done, i, n))
                ov = bC[:, :].rearrange("p (g c d) -> p g c d", c=4, d=SLOT)
                V.reciprocal(rec[:, :, :], ov[:, :, :, HD]).then_inc(c_dve, 1)
                dve.wait_ge(c_dve, level(c_dve, i, n, 1))
                dst = On[:, :].rearrange("p (g c d) -> p g c d", c=4, d=HD)
                r4 = rec[:, :, :].unsqueeze(3).to_broadcast([P, 4, 4, HD])
                t = V.tensor_tensor(dst, ov[:, :, :, 0:HD], r4, ALU.mult)
                if k != SELF:
                    t.then_inc(o_ready, 1)
                    return
                t.then_inc(c_dve, 1)
                dve.wait_ge(c_dve, level(c_dve, i, n, 2))
                V.bn_stats(st_in[:, :], On[:, :]).then_inc(c_dve, 1)
                dve.wait_ge(c_dve, level(c_dve, i, n, 3))
                dve.sem_inc(waits_carried, 1)
                V.bn_aggr(mv_in[:, :], st_in[:, :]).then_inc(c_dve, 1)

            def C1b(i, n):
                if kind_of(n) == SELF:
                    dve.wait_ge(ln_in, level(ln_in, i, n))
                    V.tensor_scalar(On2[:, :], On[:, :], mv_in[:, 0:1], rs_in[:, 1:2], ALU.subtract, ALU.mult).then_inc(o_ready, 1)

            def C3(i, n):
                k, j = kind_of(n), n % STREAMS
                dve.wait_ge(y_done, level(y_done, i, n))
                if k == ROPE:
                    t = V.tensor_tensor(X3[:, bass.ds(((i + n // STEPS) * STREAMS + j) * P, P)], bC[:, P:2 * P], XS[j][:, :], ALU.add)
                    t.then_inc(res, 1)
                    return
                dve.wait_ge(xb_done, level(xb_done, i, n))
                V.tensor_tensor(R[:, :], bC[:, P:2 * P], XB[j][:, :], ALU.add).then_inc(res, 1)

            def C4(i, n):
                if kind_of(n) != ROPE:
                    dve.wait_ge(res, level(res, i, n))
                    V.bn_stats(st_post[:, :], R[:, :]).then_inc(post, 1)

            def C5(i, n):
                if kind_of(n) != ROPE:
                    dve.wait_ge(post, level(post, i, n, 1))
                    dve.sem_inc(waits_carried, 1)
                    V.bn_aggr(mv_post[:, :], st_post[:, :]).then_inc(post, 1)

            def D(i, n):
                k, j = kind_of(n), n % STREAMS
                if k == ROPE:
                    return
                dve.wait_ge(ln_post, level(ln_post, i, n))
                V.tensor_scalar(H[j][:, :], R[:, :], mv_post[:, 0:1], rs_post[:, 4:5], ALU.subtract, ALU.mult).then_inc(h_done, 1)
                V.tensor_scalar(XS[j][:, :], R[:, :], mv_post[:, 0:1], rs_post[:, 3:4], ALU.subtract, ALU.mult).then_inc(xs_done, 1)

            def slot(i, n):
                if exists(i, n):
                    A2(i, n)
                    A2b(i, n)
                if exists(i, n - 1):
                    A4(i, n - 1, [2, 3])
                if exists(i, n - 3):
                    C3(i, n - 3)
                if exists(i, n - 1):
                    M1(i, n - 1)
                if exists(i, n - 3):
                    C4(i, n - 3)
                if exists(i, n - 1):
                    M2(i, n - 1)
                if exists(i, n - 3):
                    C5(i, n - 3)
                if exists(i, n):
                    A3(i, n)
                    mask_heads(i, n)
                if exists(i, n - 3):
                    D(i, n - 3)
                if exists(i, n - 1):
                    A5(i, n - 1)
                if exists(i, n - 2):
                    C1(i, n - 2)
                if exists(i, n):
                    A4(i, n, [0, 1])
                if exists(i, n - 2):
                    C1b(i, n - 2)

            dve.wait_ge(w_ld, W_ALL)
            dve.wait_ge(init_pool, INIT_POOL)
            V.tensor_copy(ident_b[:, :], ident[:, :])
            V.tensor_copy(mask_b[:, :, :], rep(mask_f[:, :], 4))
            for b in range(2):
                V.tensor_tensor(Kz[b][96:128, :, :], rep(ones_f[96:128, :], 4), last(slot3_one[96:128, :], P), ALU.mult)
            V.tensor_tensor(ones_r[:, :, :], rep(ones_f[:, :], 4), last(cross_one, P), ALU.mult)
            V.tensor_copy(gate_r[:, 0, :], gate_f[:, :]).then_inc(init_dve, 1)
            dve.wait_ge(init_dve, 1)
            V.tensor_tensor(gate_r[:, 1, :], gate_f[:, :], gate_r[:, 0, :].bitcast(F32), ALU.subtract)
            run_slots(dve, slot)

            def x3(i, t4):
                return X3[:, bass.ds((i * STREAMS + t4) * P, P)]

            def pre(i, b):
                for t4 in range(4):
                    V.bn_stats(st4[:, t4, :], x3(i, t4)).then_inc(pre_st, 1)
                for t4 in range(4):
                    dve.wait_ge(pre_st, level2(pre_st, i, t4 + 1))
                    dve.sem_inc(waits_carried, 1)
                    t = V.bn_aggr(mv4[:, t4, :], st4[:, t4, :])
                t.then_inc(pre_st, 1)
                dve.wait_ge(pre_st, level2(pre_st, i, 5))
                V.tensor_tensor(q4[:, :, 0:1], mv4[:, :, 0:1], mv4[:, :, 0:1], ALU.mult).then_inc(pre_q, 1)

            def pre1(i, b):
                dve.wait_ge(pre_rs, level2(pre_rs, i, 1))
                for t4 in range(4):
                    V.tensor_scalar(H2[:, t4, :], x3(i, t4), rs4[:, t4, :], None, ALU.mult).then_inc(pre_h, 1)

            def pre2(i, b):
                dve.wait_ge(pre_hi, level2(pre_hi, i, 1))
                V.scalar_tensor_tensor(hT_lo[b][:, :], bQ[:, :], norm_2, hT_hi[b][:, :].bitcast(F32), ALU.mult,
                                       ALU.subtract).then_inc(pre_lo, 1)

            def route1(i):
                dve.wait_ge(pre_g, level2(pre_g, i, 1))
                V.tensor_copy(lg[:, :, :], v3(bC[:, 0:4 * E], E)).then_inc(rt, 1)
                dve.wait_ge(rt, level2(rt, i, 1))
                dve.sem_inc(waits_carried, 1)
                for t4 in range(4):
                    V.max(top8[:, t4, :], lg[:, t4, :]).then_inc(rt, 1)

            def route1b(i):
                for t4 in range(4):
                    dve.wait_ge(rt, level2(rt, i, 2 + t4))
                    dve.sem_inc(waits_carried, 1)
                    V.max_index(idx8[:, t4, :], top8[:, t4, :], lg[:, t4, :]).then_inc(rt, 1)
                V.tensor_tensor(lg2[:, :, :], lg[:, :, :], top8[:, :, 0:1].to_broadcast([P, 4, E]), ALU.subtract
                                ).then_inc(rt, 1)

            def route2(i, b):
                dve.wait_ge(rt, level2(rt, i, 9))
                V.tensor_copy(idxf[:, :, :], idx8[:, :, :]).then_inc(rt, 1)
                dve.wait_ge(rt, level2(rt, i, 11))
                io = rep(iota_e, 4)
                V.tensor_tensor(hot[:, :, :], io, idxf[:, :, 0:1].to_broadcast([P, 4, E]), ALU.is_equal).then_inc(rt, 1)
                V.tensor_tensor(hot2[:, :, :], io, idxf[:, :, 1:2].to_broadcast([P, 4, E]), ALU.is_equal).then_inc(rt, 1)
                dve.wait_ge(rt, level2(rt, i, 13))
                V.tensor_tensor(hot[:, :, :], hot[:, :, :], hot2[:, :, :], ALU.add).then_inc(rt, 1)

            def route2b(i, b):
                dve.wait_ge(rt_exp, level2(rt_exp, i, 1))
                dve.wait_ge(rt, level2(rt, i, 14))
                V.tensor_tensor(hot2[:, :, :], hot[:, :, :], ex[:, :, :], ALU.mult).then_inc(rt, 1)
                dve.wait_ge(rt, level2(rt, i, 15))
                V.tensor_reduce(wsum[:, :, 0], hot2[:, :, :], AX.X, ALU.add).then_inc(rt, 1)
                dve.wait_ge(rt, level2(rt, i, 16))
                V.reciprocal(wrec[:, :, :], wsum[:, :, :]).then_inc(rt, 1)
                dve.wait_ge(rt, level2(rt, i, 17))
                V.scalar_tensor_tensor(Wr[b][:, :, :], hot2[:, :, :], 0.5, wrec[:, :, :].to_broadcast([P, 4, E]),
                                       ALU.mult, ALU.mult).then_inc(wr_done, 1)

            def weigh(i, b, e):
                dve.wait_ge(y2_done, level2(y2_done, i, e + 1))
                if past(i, e - 2):
                    dve.wait_ge(acc_done, level2(acc_done, i, e - 1))
                y = (bA, bO)[e % 2]
                V.tensor_tensor(yw[e % 2][:, :, :], v3(y[:, :], P), Wr[b][:, :, e % E:e % E + 1].to_broadcast([P, 4, P]),
                                ALU.mult).then_inc(yw_done, 1)

            def final1(i, b):
                dve.wait_ge(acc_done, level2(acc_done, i, E))
                for t4 in range(4):
                    V.bn_stats(st_f[:, t4, :], acc[b][:, t4, :]).then_inc(fin_st, 1)
                for t4 in range(4):
                    dve.wait_ge(fin_st, level2(fin_st, i, t4 + 1))
                    dve.sem_inc(waits_carried, 1)
                    t = V.bn_aggr(mv_f[:, t4, :], st_f[:, t4, :])
                t.then_inc(fin_st, 1)

            def final2(i, b):
                dve.wait_ge(fin_rs, level2(fin_rs, i, 2))
                if not (isinstance(i, int) and i < 2):
                    dve.wait_ge(out_done[b], 8 * (i - b))
                for t4 in range(4):
                    V.tensor_scalar(fin[b][:, t4, :], acc[b][:, t4, :], mv_f[:, t4, 0:1], rs_f[:, t4, 1:2], ALU.subtract,
                                    ALU.mult).then_inc(fin_done, 1)

            def experts(i, b, more):
                first = isinstance(i, int) and i == 0
                for u in range(n_units):
                    dve.wait_ge(tanh_done, level2(tanh_done, i, u + 1))
                    V.scalar_tensor_tensor(sg[u % 2][:, :], th[u % 2][:, :], 1.0, bS[u % 2][:, :], ALU.add, ALU.mult
                                           ).then_inc(sg_done, 1)
                    dve.wait_ge(sg_done, level2(sg_done, i, u + 1))
                    if past(i, u - 4):
                        dve.wait_ge(y2_done, level2(y2_done, i, (u - 4) // FC + 1))
                    V.tensor_tensor(G[u % 4][:, :], sg[u % 2][:, :], bT[u % 2][:, :], ALU.mult).then_inc(g_done, 1)
                    e = u // FC - 2
                    if u % FC == 0 and (e >= 0 or not first):
                        weigh(i, b if e >= 0 else 1 - b, e)
                    if more:
                        if u == 3:
                            pre(i + 1, 1 - b)
                        if u == 5:
                            pre1(i + 1, 1 - b)
                        if u == 8:
                            pre2(i + 1, 1 - b)
                        if u == 10:
                            route1(i + 1)
                        if u == 11:
                            route1b(i + 1)
                        if u == 13:
                            route2(i + 1, 1 - b)
                        if u == 14:
                            route2b(i + 1, 1 - b)
                    if not first and u == 6:
                        final1(i - 1, 1 - b)
                    if not first and u == 9:
                        final2(i - 1, 1 - b)
                if not more:
                    weigh(i, b, E - 2)
                    weigh(i, b, E - 1)

            pre(0, 0)
            pre1(0, 0)
            pre2(0, 0)
            route1(0)
            route1b(0)
            route2(0, 0)
            route2b(0, 0)
            run_groups(dve, experts)
            final1(ITER - 1, 1)
            final2(ITER - 1, 1)

        @block.gpsimd
        def _(pool):
            G_ = nc.gpsimd

            def xb(i, n):
                k, j = kind_of(n), n % STREAMS
                if k == ROPE:
                    return
                if k == SELF:
                    pool.wait_ge(x_ld[j], 16 * (i + 1))
                    if exists(i, n - STREAMS):
                        pool.wait_ge(res, level(res, i, n - STREAMS))
                else:
                    pool.wait_ge(xs_done, level(xs_done, i, n - STREAMS))
                src = XL[j] if k == SELF else XS[j]
                G_.tensor_tensor(XB[j][:, :], src[:, :], b_out[k], ALU.add).then_inc(xb_done, 1)

            def kz(i, n):
                b = n % 2
                if kind_of(n) == CROSS:
                    pool.wait_ge(lo_done, level(lo_done, i, n))
                    G_.tensor_tensor(Qlo[b][:, :, :], rep(c_lo[:, 0, :].bitcast(F32), 4), last(same_c, P), ALU.mult)
                    G_.tensor_tensor(Klo[b][:, :, :], rep(c_lo[:, 1, :].bitcast(F32), 4), last(same_r, P), ALU.mult).then_inc(kz_pool, 1)

            def sel(i, n, cs):
                if kind_of(n) == CROSS:
                    return
                for c in cs:
                    pool.wait_ge(exp_done, level(exp_done, i, n, c + 1))
                    pool.sem_inc(waits_carried, 1)
                    G_.affine_select(out=v3(PT[c][:, :], P), in_=v3(PT[c][:, :], P), pattern=[[0, 4], [1, P]],
                                         compare_op=ALU.is_ge, fill=0.0, base=0, channel_multiplier=-1).then_inc(causal, 1)

            def rs_inner(i, n):
                if kind_of(n) != SELF:
                    return
                pool.wait_ge(c_dve, level(c_dve, i, n))
                G_.tensor_tensor(rs_in[:, 0:1], mv_in[:, 1:2], eps_col, ALU.add).then_inc(ln_in, 1)
                pool.wait_ge(ln_in, level(ln_in, i, n, 1))
                G_.tensor_tensor(rs_in[:, 1:2], rs_in[:, 0:1], minus_half, ALU.pow).then_inc(ln_in, 1)

            def rs_after(i, n):
                if kind_of(n) == ROPE:
                    pool.wait_ge(res, level(res, i, n))
                    col = bass.ds(((i + n // STEPS) * STREAMS + n % STREAMS) * P, P)
                    G_.tensor_tensor(X23[:, col], X3[:, col], XS[n % STREAMS][:, :], ALU.add).then_inc(xb_done, 1)
                    return
                pool.wait_ge(post, level(post, i, n))
                G_.tensor_tensor(rs_post[:, 0:1], mv_post[:, 1:2], eps_col, ALU.add).then_inc(ln_post, 1)
                pool.wait_ge(ln_post, level(ln_post, i, n, 1))
                G_.tensor_tensor(rs_post[:, 2:3], rs_post[:, 0:1], eps_col, ALU.mult).then_inc(ln_post, 1)
                pool.wait_ge(ln_post, level(ln_post, i, n, 2))
                G_.tensor_tensor(rs_post[:, 1:2], rs_post[:, 2:3], mv_post[:, 1:2], ALU.add).then_inc(ln_post, 1)
                pool.wait_ge(ln_post, level(ln_post, i, n, 3))
                G_.tensor_tensor(rs_post[:, 3:5], rs_post[:, 0:2], minus_half.to_broadcast([P, 2]), ALU.pow).then_inc(ln_post, 1)

            def slot(i, n):
                if exists(i, n - 2):
                    sel(i, n - 2, [0, 1, 2, 3])
                if exists(i, n):
                    xb(i, n)
                if exists(i, n - 3):
                    rs_after(i, n - 3)
                if exists(i, n):
                    kz(i, n)
                if exists(i, n - 2):
                    rs_inner(i, n - 2)

            def split_w13(c):
                col = slice(CHUNK * c, CHUNK * c + CHUNK)
                pool.wait_ge(w13_high, c + 1)
                G_.tensor_tensor(w13_lo[:, col], w13_f[:, col], w13_hi[:, col].bitcast(F32), ALU.subtract).then_inc(w13_split, 1)

            G_.memset(MxG[:, :, :], 0.0)
            G_.memset(MxC[:, :, :], 0.0)
            G_.memset(ones_f[:, :], 1.0)
            for b in range(3):
                G_.memset(VG[b][:, :, :], 0.0)
                G_.memset(VC[b][:, :, :], 0.0)
            pool_set = G_.memset(rs_in[:, :], 0.0)
            pool_set.then_inc(pool_zero, 1)
            pool.wait_ge(pool_zero, 1)
            for b in range(3):
                G_.memset(VG[b][:, :, HD:HD + 1], 1.0)
                t = G_.memset(VC[b][:, :, HD:HD + 1], 1.0)
            t.then_inc(init_pool, 1)
            pool.wait_ge(w_ld, W_ALL)
            run_slots(pool, slot, split_w13)

            def pre(i):
                pool.wait_ge(pre_q, level2(pre_q, i, 1))
                G_.tensor_tensor(q4[:, :, 1:2], q4[:, :, 0:1], mv4[:, :, 1:2], ALU.add).then_inc(pre_pool, 1)
                pool.wait_ge(pre_pool, level2(pre_pool, i, 1))
                G_.tensor_tensor(q4[:, :, 0:1], q4[:, :, 1:2], rep(eps_col, 4), ALU.add).then_inc(pre_pool, 1)
                pool.wait_ge(pre_pool, level2(pre_pool, i, 2))
                G_.tensor_tensor(rs4[:, :, :], q4[:, :, 0:1], rep(minus_half, 4), ALU.pow).then_inc(pre_rs, 1)

            def accumulate(i, b, e):
                pool.wait_ge(yw_done, level2(yw_done, i, e + 1))
                if e == 0:
                    if not (isinstance(i, int) and i < 2):
                        pool.wait_ge(fin_done, level2(fin_done, i - 2, 4))
                    src = v3(X23[:, bass.ds(i * N, N)], P)
                else:
                    pool.wait_ge(acc_done, level2(acc_done, i, e))
                    src = acc[b][:, :, :]
                G_.tensor_tensor(acc[b][:, :, :], src, yw[e % 2][:, :, :], ALU.add).then_inc(acc_done, 1)

            def final(i):
                pool.wait_ge(fin_st, level2(fin_st, i, 5))
                G_.tensor_tensor(rs_f[:, :, 0:1], mv_f[:, :, 1:2], rep(eps_col, 4), ALU.add).then_inc(fin_rs, 1)
                pool.wait_ge(fin_rs, level2(fin_rs, i, 1))
                G_.tensor_tensor(rs_f[:, :, 1:2], rs_f[:, :, 0:1], rep(minus_half, 4), ALU.pow).then_inc(fin_rs, 1)

            def experts(i, b, more):
                first = isinstance(i, int) and i == 0
                if not first:
                    accumulate(i, 1 - b, -2)
                    accumulate(i, 1 - b, -1)
                if more:
                    pre(i + 1)
                if not first:
                    final(i - 1)
                for e in range(E if not more else E - 2):
                    accumulate(i, b, e)

            pre(0)
            pool.wait_ge(xb_done, level(xb_done, ITER, -1))
            run_groups(pool, experts)
            final(ITER - 1)



def kernel(**inputs):
    import numpy as np
    import concourse.bacc as bacc
    from concourse.bass_utils import run_bass_kernel_spmd as run

    a = {k: np.asarray(v) for k, v in inputs.items()}
    C = np.ascontiguousarray
    f = np.float32
    T = 128

    def q_order(w):
        return w.reshape(4, 4, 8, -1).transpose(1, 0, 2, 3).reshape(128, -1)

    wqkv = a["L0_ffn_wqkv"]
    w_rope = np.concatenate([q_order(wqkv[:128]), wqkv[128:]], axis=0).T
    wo_rope = q_order(a["L0_ffn_wo"].T)
    rows = np.concatenate([a[k] for k in ("L0_attn_bq", "L0_attn_bk", "L0_attn_bv", "L0_xattn_b_q", "L0_xattn_b_kv",
                                          "L0_attn_bo", "L0_xattn_b_out")])
    feat = np.stack([a[k] for k in ("L0_attn_ln_g", "L0_attn_ln_b", "L0_xattn_w_norm", "L0_ffn_ln1_w", "L0_ffn_ln2_w")], axis=1)

    p = np.arange(128)
    k4 = np.arange(4)
    same_c = ((p % 32) // 8)[:, None] == k4
    same_r = (p // 32)[:, None] == k4
    inv_freq = f(1.0) / (f(10000.0) ** (np.arange(0, 8, 2, dtype=f) / f(8)))
    ang = np.arange(T, dtype=f)[:, None] * inv_freq[None, :]
    cos, sin = np.cos(ang), np.sin(ang)
    two = (p % 8 < 2)[:, None]
    tables = np.concatenate([same_c, same_r, cos, cos, -sin, sin, same_c & two, same_r & two,
                             np.tile(np.arange(8), (128, 1)), np.full((128, 1), -0.5), np.full((128, 1), EPS)], axis=1).astype(f)
    mask = np.where(p[None, :] > p[:, None], f(NEG), f(0)).astype(f)

    E = a["L0_ffn_gate_w"].shape[0]
    arrays = {
        "x": a["x"],
        "ctx_in": a["ctx_1024"],
        "w_self": np.concatenate([a["L0_attn_Wq"], a["L0_attn_Wk"], a["L0_attn_Wv"]], axis=1),
        "w_crossq": a["L0_xattn_w_q"].T,
        "w_crosskv": a["L0_xattn_w_kv"].T,
        "w_rope": w_rope,
        "w_out": np.stack([a["L0_attn_Wo"], a["L0_xattn_w_out"].T, wo_rope]),
        "bias_rows": np.broadcast_to(rows, (128, rows.size)),
        "feat_cols": feat,
        "tables": tables,
        "ident_in": np.eye(128, dtype=f),
        "mask_in": mask,
        "gate_in": a["L0_ffn_gate_w"].T,
        "w13_in": a["L0_ffn_w13"].transpose(2, 0, 1).reshape(128, -1),
        "w2_in": a["L0_ffn_w2"].reshape(E, 128, -1, 128).transpose(3, 0, 2, 1).reshape(128, -1),
    }
    nc = bacc.Bacc("TRN2", target_bir_lowering=False, num_devices=1)
    arrays = {k: C(v) for k, v in arrays.items()}
    aps = [nc.dram_tensor(k, v.shape, mybir.dt.from_np(v.dtype), kind="ExternalInput").ap() for k, v in arrays.items()]
    out = nc.dram_tensor("out", a["x"].shape, F32, kind="ExternalOutput").ap()
    program(nc, *aps, out)
    r = run(nc, [arrays], core_ids=[0])
    return r.results[0]["out"]
```

```python
from contextlib import ExitStack

import concourse.bass as bass
from concourse import mybir

P = 128
F32 = mybir.dt.float32
F32R = mybir.dt.float32r
BF16 = mybir.dt.bfloat16
U32 = mybir.dt.uint32
ALU = mybir.AluOpType
ACT = mybir.ActivationFunctionType
AX = mybir.AxisListType

HD = 8
SLOT = 32
NEG = -1e30
EPS = 1e-5
SCALE = HD ** -0.5
STREAMS = 8
GROUP = 4
KINDS = 3
STEPS = STREAMS * KINDS
SELF, CROSS, ROPE = range(KINDS)


def kind_of(n):
    return (n % STEPS) // STREAMS


def program(nc, x, ctx_in, w_self, w_crossq, w_crosskv, w_rope, w_out, bias_rows, feat_cols, tables, ident_in,
            mask_in, gate_in, w13_in, w2_in, out):
    NB = x.shape[0]
    ITER = NB // STREAMS
    E = gate_in.shape[1]
    F = w13_in.shape[1] // (2 * E)
    FC = F // P
    GROUPS = NB // GROUP
    N = GROUP * P

    with ExitStack() as ctx:
        def sb(name, shape, dt=F32):
            return ctx.enter_context(nc.sbuf_tensor(name, shape, dt))

        def ps(name):
            return ctx.enter_context(nc.psum_tensor(name, [P, 512], F32))

        def sem(name):
            return ctx.enter_context(nc.semaphore(name))

        Wself = sb("Wself", [P, 192])
        Wcq = sb("Wcq", [P, P])
        Wckv = sb("Wckv", [P, 2 * P])
        Wrope = sb("Wrope", [P, 192])
        Wout = sb("Wout", [P, KINDS, P])
        bias = sb("bias", [P, 832])
        b_self, b_cross = bias[:, 0:192], bias[:, 192:576]
        b_out = [bias[:, 576:704], bias[:, 704:832]]
        feat = sb("feat", [P, 5])
        ln_g, ln_b, norm_x, norm_1, norm_2 = [feat[:, k:k + 1] for k in range(5)]
        tab = sb("tab", [P, 4 + 4 + 8 + 8 + 4 + 4 + 8 + 1 + 1])
        same_c, cos_t, sin_t = tab[:, 0:4], tab[:, 8:16], tab[:, 16:24]
        slot3_one, max_one, iota_e, minus_half, eps_col = tab[:, 24:28], tab[:, 28:32], tab[:, 32:40], tab[:, 40:41], tab[:, 41:42]
        ident = sb("ident", [P, P])
        ident_b = sb("ident_b", [P, P], BF16)
        mask_f = sb("mask_f", [P, P])
        mask_b = sb("mask_b", [P, 4, P], BF16)
        ones_f = sb("ones_f", [P, P])
        gate_f = sb("gate_f", [P, E])
        gate_r = sb("gate_r", [P, 2, E], F32R)
        w13_f = sb("w13_f", [P, 2 * E * F])
        w13_hi = sb("w13_hi", [P, 2 * E * F], F32R)
        w13_lo = sb("w13_lo", [P, 2 * E * F], F32R)
        w2_f = sb("w2_f", [P, E * FC * P])

        XL = [sb(f"XL{j}", [P, P]) for j in range(STREAMS)]
        CL = [sb(f"CL{j}", [P, P]) for j in range(STREAMS)]
        XS = [sb(f"XS{j}", [P, P]) for j in range(STREAMS)]
        H = [sb(f"H{j}", [P, P]) for j in range(STREAMS)]
        XB = [sb(f"XB{j}", [P, P]) for j in range(STREAMS)]
        xTs = sb("xTs", [P, P])
        cTs = sb("cTs", [P, P])
        T = sb("T", [P, 2 * P])
        T3 = sb("T3", [P, 5, 3, SLOT])
        rope1 = sb("rope1", [P, 20, HD])
        rope2 = sb("rope2", [P, 20, HD])
        VG = [sb(f"VG{b}", [P, 4, SLOT]) for b in range(3)]
        VC = [sb(f"VC{b}", [P, 16, SLOT]) for b in range(3)]
        Qs = [sb(f"Qs{b}", [P, 512], F32R) for b in range(2)]
        K1 = sb("K1", [P, P], F32R)
        Kz = [sb(f"Kz{b}", [P, 4, P], F32R) for b in range(2)]
        c_hi = sb("c_hi", [P, 2, P], F32R)
        c_lo = sb("c_lo", [P, 2, P], F32R)
        Qhm = [[sb(f"Qhm{b}_{u}", [P, 4, P], F32R) for u in range(2)] for b in range(2)]
        Qlo = [sb(f"Qlo{b}", [P, 4, P], F32R) for b in range(2)]
        Khi = [sb(f"Khi{b}", [P, 4, P], F32R) for b in range(2)]
        Klo = [sb(f"Klo{b}", [P, 4, P], F32R) for b in range(2)]
        negmax = sb("negmax", [P, 4, 4])
        MxG = sb("MxG", [P, 4, SLOT])
        MxC = sb("MxC", [P, 16, HD])
        PT = [sb(f"PT{c}", [P, 512]) for c in range(4)]
        OTs = sb("OTs", [P, 512])
        rec = sb("rec", [P, 4, 4])
        On = sb("On", [P, P])
        On2 = sb("On2", [P, P])
        OnT = sb("OnT", [P, P])
        R = sb("R", [P, P])
        st_in = sb("st_in", [P, 6])
        mv_in = sb("mv_in", [P, 2])
        rs_in = sb("rs_in", [P, 2])
        st_post = sb("st_post", [P, 6])
        mv_post = sb("mv_post", [P, 2])
        rs_post = sb("rs_post", [P, 6])
        X3 = sb("X3", [P, NB * P])
        X23 = sb("X23", [P, NB * P])

        st4 = sb("st4", [P, 4, 6])
        mv4 = sb("mv4", [P, 4, 2])
        q4 = sb("q4", [P, 4, 2])
        rs4 = sb("rs4", [P, 4, 1])
        H2 = sb("h_moe", [P, 4, P])
        hT_hi = [sb(f"hT_hi{b}", [P, N], F32R) for b in range(2)]
        hT_lo = [sb(f"hT_lo{b}", [P, N], F32R) for b in range(2)]
        lg = sb("lg", [P, 4, E])
        top8 = sb("top8", [P, 4, 8])
        idx8 = sb("idx8", [P, 4, 8], U32)
        idxf = sb("idxf", [P, 4, 8])
        lg2 = sb("lg2", [P, 4, E])
        ex = sb("ex", [P, 4, E])
        hot = sb("hot", [P, 4, E])
        hot2 = sb("hot2", [P, 4, E])
        wsum = sb("wsum", [P, 4, 1])
        wrec = sb("wrec", [P, 4, 1])
        Wr = [sb(f"Wr{b}", [P, 4, E]) for b in range(2)]
        th = [VC[b][:, :, :].rearrange("p a b -> p (a b)") for b in range(2)]
        sg = [VC[2][:, :, :].rearrange("p a b -> p (a b)"), OTs]
        G = PT
        yw = [sb(f"yw{b}", [P, 4, P]) for b in range(2)]
        acc = [sb(f"acc{b}", [P, 4, P]) for b in range(2)]
        st_f = sb("st_f", [P, 4, 6])
        mv_f = sb("mv_f", [P, 4, 2])
        rs_f = sb("rs_f", [P, 4, 2])
        fin = [sb(f"fin{b}", [P, 4, P]) for b in range(2)]

        bA, bQ, bC, bS0, bS1, bT0, bT1, bO = [ps(f"bank{k}") for k in range(8)]
        bS, bT = [bS0, bS1], [bT0, bT1]

        w_ld = sem("w_ld")
        w_more = sem("w_more")
        x_ld = [sem(f"x_ld{j}") for j in range(STREAMS)]
        c_ld = [sem(f"c_ld{j}") for j in range(STREAMS)]
        w13_ld = sem("w13_ld")
        init_pool = sem("init_pool")
        gate_done = sem("gate_done")
        init_dve = sem("init_dve")
        w13_high = sem("w13_high")
        waits_carried = sem("waits_carried")

        CHUNK = 512
        CHUNKS = 2 * E * F // CHUNK
        W_FIRST, W_MORE = 16 * 5, 16 * 6
        per_step = {}

        def step_sem(name, *counts):
            s = sem(name)
            per_step[s] = counts if len(counts) > 1 else counts * KINDS
            return s

        xT_done = step_sem("xT_done", 1)
        xT_evac = step_sem("xT_evac", 1)
        qkv_done = step_sem("qkv_done", 1)
        tok = step_sem("tok", 1, 1, 4)
        qkT_done = step_sem("qkT_done", 1)
        hi_done = step_sem("hi_done", 1)
        lo_done = step_sem("lo_done", 1)
        kz_done = step_sem("kz_done", 1)
        kz_pool = step_sem("kz_pool", 0, 2, 0)
        klo_done = step_sem("klo_done", 0, 1, 0)
        s_done = step_sem("s_done", 4)
        s_max = step_sem("s_max", 4)
        m_hi = step_sem("m_hi", 1)
        m_done = step_sem("m_done", 1)
        mT_done = step_sem("mT_done", 1)
        m_evac = step_sem("m_evac", 1)
        m_evac_up = step_sem("m_evac_up", 0, 1, 0)
        st_done = step_sem("st_done", 4)
        exp_done = step_sem("exp_done", 4)
        causal = step_sem("causal", 4, 0, 4)
        pv_done = step_sem("pv_done", 1)
        ot_evac = step_sem("ot_evac", 1)
        on_done = step_sem("on_done", 1)
        c_dve = step_sem("c_dve", 4, 1, 1)
        ln_in = step_sem("ln_in", 2, 0, 0)
        o_ready = step_sem("o_ready", 1)
        oT_done = step_sem("oT_done", 1)
        oT_evac = step_sem("oT_evac", 1)
        y_done = step_sem("y_done", 1)
        xb_done = step_sem("xb_done", 1, 1, 0)
        x23_done = step_sem("x23_done", 0, 0, 1)
        res = step_sem("res", 1)
        post = step_sem("post", 2, 2, 0)
        ln_post = step_sem("ln_post", 4, 4, 0)
        xs_done = step_sem("xs_done", 1, 1, 0)
        h_done = step_sem("h_done", 1, 1, 0)

        def level(s, i, n, m=None):
            counts = per_step[s]
            i, n = i + n // STEPS, n % STEPS
            if m is None:
                m = counts[kind_of(n)]
            return i * STREAMS * sum(counts) + sum(counts[kind_of(a)] for a in range(n)) + m

        def exists(i, n):
            if not isinstance(i, int):
                return True
            return 0 <= i * STEPS + n < ITER * STEPS

        def v3(ap, b):
            return ap.rearrange("p (a b) -> p a b", b=b)

        def rep(ap, k):
            return ap.unsqueeze(1).to_broadcast([ap.shape[0], k, ap.shape[1]])

        def last(ap, k):
            return ap.unsqueeze(2).to_broadcast([ap.shape[0], ap.shape[1], k])

        def thrice(ap):
            return v3(ap, SLOT).unsqueeze(2).to_broadcast([P, 5, 3, SLOT])

        block = ctx.enter_context(nc.Block())

        per_group = {}

        def p2(name, per_iter):
            s = sem(name)
            per_group[s] = per_iter
            return s

        w13_split = sem("w13_split")
        n_units = E * FC
        pre_st = p2("pre_st", 5)
        pre_q = p2("pre_q", 1)
        pre_rs = p2("pre_rs", 1)
        pre_h = p2("pre_h", 4)
        pre_t = p2("pre_t", 1)
        pre_hi = p2("pre_hi", 1)
        pre_lo = p2("pre_lo", 1)
        pre_g = p2("pre_g", 1)
        rt = p2("rt", 17)
        rt_exp = p2("rt_exp", 1)
        xu_done = p2("xu_done", n_units)
        tanh_done = p2("tanh_done", n_units)
        sg_done = p2("sg_done", n_units)
        g_done = p2("g_done", n_units)
        y2_done = p2("y2_done", E)
        yw_done = p2("yw_done", E)
        acc_done = p2("acc_done", E)
        fin_st = p2("fin_st", 5)
        fin_rs = p2("fin_rs", 2)
        fin_done = p2("fin_done", 4)
        wr_done = p2("wr_done", 1)
        pre_pool = p2("pre_pool", 2)
        pool_zero = sem("pool_zero")
        out_done = [sem(f"out_done{b}") for b in range(2)]

        def level2(s, i, m):
            return i * per_group[s] + m

        def past(i, k):
            return not isinstance(i, int) or i > 0 or k >= 0

        @block.sync
        def _(sp):
            def load(i, which):
                for j in range(STREAMS):
                    b = i * STREAMS + j
                    if which == "x":
                        if not (isinstance(i, int) and i == 0):
                            sp.wait_ge(xT_done, level(xT_done, i - 1, j))
                            sp.sem_inc(waits_carried, 1)
                            sp.wait_ge(xb_done, level(xb_done, i - 1, j))
                            sp.sem_inc(waits_carried, 1)
                        sp.dma_start(XL[j][:, :], x[bass.ds(b, 1), :, :].rearrange("b s d -> (b s) d")
                                     ).then_inc(x_ld[j], 16)
                    else:
                        if not (isinstance(i, int) and i == 0):
                            sp.wait_ge(xT_done, level(xT_done, i - 1, STREAMS + j))
                            sp.sem_inc(waits_carried, 1)
                        sp.dma_start(CL[j][:, :], ctx_in[bass.ds(b, 1), :, :].rearrange("b s d -> (b s) d")
                                     ).then_inc(c_ld[j], 16)

            sp.dma_start(ident[:, :], ident_in).then_inc(w_ld, 16)
            sp.dma_start(XL[0][:, :], x[0, :, :]).then_inc(x_ld[0], 16)
            sp.dma_start(Wself[:, :], w_self).then_inc(w_ld, 16)
            sp.dma_start(mask_f[:, :], mask_in).then_inc(w_ld, 16)
            sp.dma_start(tab[:, :], tables).then_inc(w_ld, 16)
            sp.dma_start(bias[:, :], bias_rows).then_inc(w_ld, 16)
            sp.dma_start(XL[1][:, :], x[1, :, :]).then_inc(x_ld[1], 16)
            sp.dma_start(feat[:, :], feat_cols).then_inc(w_more, 16)
            sp.dma_start(Wout[:, :, :], w_out.rearrange("k p n -> p k n")).then_inc(w_more, 16)
            sp.dma_start(Wcq[:, :], w_crossq).then_inc(w_more, 16)
            sp.dma_start(Wckv[:, :], w_crosskv).then_inc(w_more, 16)
            sp.dma_start(Wrope[:, :], w_rope).then_inc(w_more, 16)
            sp.dma_start(gate_f[:, :], gate_in).then_inc(w_more, 16)
            for j in range(2, STREAMS):
                sp.dma_start(XL[j][:, :], x[j, :, :]).then_inc(x_ld[j], 16)
            load(0, "c")
            sp.dma_start(w13_f[:, :], w13_in).then_inc(w13_ld, 16)
            sp.dma_start(w2_f[:, :], w2_in).then_inc(w13_ld, 16)
            with sp.Fori(1, ITER) as i:
                load(i, "x")
                load(i, "c")

            def store(i, b):
                sp.wait_ge(fin_done, level2(fin_done, i, 4))
                sp.sem_inc(waits_carried, 1)
                sp.dma_start(out[bass.ds(i * GROUP, GROUP), :, :].rearrange("b s d -> s b d"),
                             fin[b][:, :, :]).then_inc(out_done[b], 16)

            with sp.Fori(0, GROUPS // 2) as h:
                for b in range(2):
                    store(h * 2 + b, b)
            for b in range(2):
                sp.wait_ge(out_done[b], 16 * (GROUPS // 2))


        def run_slots(eng, slot, once=None):
            for n in range(STEPS):
                slot(0, n)
                if once:
                    once(n)
            with eng.Fori(1, ITER) as i:
                for n in range(STEPS):
                    slot(i, n)
            for n in range(6):
                slot(ITER, n)

        def run_groups(eng, body):
            body(0, 0, True)
            body(1, 1, True)
            with eng.Fori(1, GROUPS // 2 - 1) as h:
                body(h * 2, 0, True)
                body(h * 2 + 1, 1, True)
            body(GROUPS - 2, 0, True)
            body(GROUPS - 1, 1, False)

        INIT_V, INIT_KZ, INIT_CROSS = 1, 2, 3


        @block.tensor
        def _(pe):
            mm = nc.tensor.matmul

            def A1(i, n):
                k, j = kind_of(n), n % STREAMS
                if k == SELF:
                    pe.wait_ge(x_ld[j], 16 * (i + 1))
                else:
                    pe.wait_ge(h_done, level(h_done, i, n - STREAMS))
                if exists(i, n - 1):
                    pe.wait_ge(lo_done, level(lo_done, i, n - 1))
                src = XL[j] if k == SELF else H[j]
                t = nc.tensor.transpose(bA[:, 0:P], src[:, :], ident[:, :])
                if k == CROSS:
                    pe.wait_ge(c_ld[j], 16 * (i + 1))
                    t = nc.tensor.transpose(bA[:, 2 * P:3 * P], CL[j][:, :], ident[:, :])
                t.then_inc(xT_done, 1)

            def A2(i, n):
                k = kind_of(n)
                pe.wait_ge(xT_evac, level(xT_evac, i, n))
                if k == CROSS:
                    mm(bA[:, P:2 * P], xTs[:, :], Wcq[:, :], start=True, stop=True)
                    t = mm(bA[:, 2 * P:4 * P], cTs[:, :], Wckv[:, :], start=True, stop=True)
                else:
                    t = mm(bA[:, P:P + 192], xTs[:, :], (Wself if k == SELF else Wrope)[:, :], start=True, stop=True)
                t.then_inc(qkv_done, 1)

            def A3(i, n):
                k = kind_of(n)
                pe.wait_ge(tok, level(tok, i, n))
                if k == CROSS:
                    nc.tensor.transpose(bQ[:, 0:P], T[:, 0:P], ident[:, :])
                    t = nc.tensor.transpose(bA[:, 0:P], T[:, P:2 * P], ident[:, :])
                else:
                    for g in range(4):
                        nc.tensor.transpose(bQ[0:96, P * g:P * g + P], T3[:, g, :, :], ident[:, :])
                    t = nc.tensor.transpose(bA[0:96, 0:P], T3[:, 4, :, :], ident[:, :])
                t.then_inc(qkT_done, 1)

            def A4(i, n, gs):
                k, b = kind_of(n), n % 2
                if 0 in gs:
                    pe.wait_ge(kz_done, level(kz_done, i, n))
                    if k == CROSS:
                        pe.wait_ge(kz_pool, level(kz_pool, i, n, 1))
                for g in gs:
                    if exists(i, n - 1) or g >= 2:
                        pe.wait_ge(s_max, level(s_max, i, n, g - 1))
                    if g == 1 and exists(i, n - 1):
                        pe.wait_ge(m_evac, level(m_evac, i, n - 1))
                        if kind_of(n - 1) == CROSS:
                            pe.wait_ge(m_evac_up, level(m_evac_up, i, n - 1))
                    if k == CROSS:
                        mm(bS[g % 2][:, 0:2 * P], Qhm[b][1][:, g, :], Khi[b][:, 2:4, :], start=True, stop=True)
                        t = mm(bS[g % 2][:, 2 * P:4 * P], Qhm[b][0][:, g, :], Khi[b][:, 0:2, :], start=True, stop=True)
                    else:
                        mm(bS[g % 2][:, :], Qs[b][0:96, P * g:P * g + P], Kz[b][0:96, :, :], start=True, stop=False)
                        t = mm(bS[g % 2][:, :], ident_b[:, :], mask_b[:, :, :], start=False, stop=True)
                    t.then_inc(s_done, 1)

            def A5(i, n):
                k = kind_of(n)
                pe.wait_ge(m_done, level(m_done, i, n))
                if k == CROSS:
                    t = nc.tensor.transpose(bS1[:, 0:P], MxC[:, :, :], ident[:, :])
                else:
                    t = nc.tensor.transpose(bS1[:, 0:P], MxG[:, :, :], ident[:, :])
                t.then_inc(mT_done, 1)

            def B1(i, n, cs):
                k, b = kind_of(n), n % 2
                if 0 in cs:
                    pe.wait_ge(m_evac, level(m_evac, i, n))
                    if k == CROSS:
                        pe.wait_ge(m_evac_up, level(m_evac_up, i, n))
                        pe.wait_ge(kz_pool, level(kz_pool, i, n))
                        pe.wait_ge(klo_done, level(klo_done, i, n))
                for c in cs:
                    if exists(i, n - 1) or c >= 2:
                        pe.wait_ge(exp_done, level(exp_done, i, n, c - 1))
                    o = bT[c % 2][:, :]
                    if k == CROSS:
                        mm(o, Khi[b][:, c, :], Qhm[b][c // 2][:, :, :], start=True, stop=False)
                        mm(o, Khi[b][:, c, :], Qlo[b][:, :, :], start=False, stop=False)
                        t = mm(o, Klo[b][:, c, :], Qhm[b][c // 2][:, :, :], start=False, stop=True)
                    else:
                        t = mm(o, Kz[b][:, c, :], Qs[b][:, :], start=True, stop=True)
                    t.then_inc(st_done, 1)

            def B2(i, n):
                k, b = kind_of(n), n % 2
                if exists(i, n - 1):
                    pe.wait_ge(ot_evac, level(ot_evac, i, n - 1))
                for c in range(4):
                    if k == CROSS:
                        pe.wait_ge(exp_done, level(exp_done, i, n, c + 1))
                        for h in range(4):
                            t = mm(bO[SLOT * h:SLOT * h + SLOT, P * c:P * c + P], VC[n % 3][:, 4 * c + h, :],
                                   PT[c][:, P * h:P * h + P], start=True, stop=True, tile_position=(0, SLOT * h))
                    else:
                        pe.wait_ge(causal, level(causal, i, n, c + 1))
                        t = mm(bO[SLOT * c:SLOT * c + SLOT, :], VG[n % 3][:, c, :], PT[c][:, :], start=True, stop=True,
                               tile_position=(0, SLOT * c))
                t.then_inc(pv_done, 1)

            def C1(i, n):
                pe.wait_ge(ot_evac, level(ot_evac, i, n))
                if exists(i, n - 1):
                    pe.wait_ge(res, level(res, i, n - 1))
                for g in range(4):
                    t = nc.tensor.transpose(v3(bC[:, :], P)[:, g, :], OTs[:, P * g:P * g + P], ident[:, :])
                t.then_inc(on_done, 1)

            def C2(i, n):
                pe.wait_ge(o_ready, level(o_ready, i, n))
                t = nc.tensor.transpose(bC[:, 0:P], (On2 if kind_of(n) == SELF else On)[:, :], ident[:, :])
                t.then_inc(oT_done, 1)

            def C3(i, n):
                pe.wait_ge(oT_evac, level(oT_evac, i, n))
                mm(bC[:, P:2 * P], OnT[:, :], Wout[:, kind_of(n), :], start=True, stop=True).then_inc(y_done, 1)

            def slot(i, n):
                if exists(i, n - 3):
                    B1(i, n - 3, [1])
                if exists(i, n - 1):
                    A2(i, n - 1)
                if exists(i, n - 3):
                    B1(i, n - 3, [2])
                if exists(i, n - 2):
                    A4(i, n - 2, [2])
                if exists(i, n - 5):
                    C2(i, n - 5)
                if exists(i, n - 2):
                    A4(i, n - 2, [3])
                if exists(i, n - 3):
                    B1(i, n - 3, [3])
                if exists(i, n - 1):
                    A3(i, n - 1)
                if exists(i, n - 5):
                    C3(i, n - 5)
                if exists(i, n - 4):
                    C1(i, n - 4)
                if exists(i, n - 2):
                    A5(i, n - 2)
                if exists(i, n - 3):
                    B2(i, n - 3)
                if exists(i, n):
                    A1(i, n)
                if exists(i, n - 2):
                    B1(i, n - 2, [0])
                if exists(i, n - 1):
                    A4(i, n - 1, [0, 1])

            def once(n):
                if n == 0:
                    pe.wait_ge(init_pool, INIT_KZ)
                    pe.wait_ge(init_dve, 1)
                if n == 2:
                    pe.wait_ge(init_pool, INIT_CROSS)
                    pe.wait_ge(w_more, W_MORE)

            pe.wait_ge(w_ld, W_FIRST)
            run_slots(pe, slot, once)

            def pre(i):
                pe.wait_ge(pre_h, level2(pre_h, i, 4))
                for t4 in range(4):
                    t = nc.tensor.transpose(v3(bQ[:, :], P)[:, t4, :], H2[:, t4, :], ident[:, :])
                t.then_inc(pre_t, 1)

            def router(i, b):
                pe.wait_ge(pre_lo, level2(pre_lo, i, 1))
                for t4 in range(4):
                    o = bC[:, E * t4:E * t4 + E]
                    lh, ll = hT_hi[b][:, P * t4:P * t4 + P], hT_lo[b][:, P * t4:P * t4 + P]
                    mm(o, lh, gate_r[:, 0, :], start=True, stop=False)
                    mm(o, lh, gate_r[:, 1, :], start=False, stop=False)
                    t = mm(o, ll, gate_r[:, 0, :], start=False, stop=True)
                t.then_inc(pre_g, 1)

            def unit(i, b, u):
                e, f = u // FC, u % FC
                for w in range(2):
                    o = (bS if w == 0 else bT)[u % 2][:, :]
                    if past(i, u - 2):
                        if w == 0:
                            pe.wait_ge(sg_done, level2(sg_done, i, u - 1))
                        else:
                            pe.wait_ge(g_done, level2(g_done, i, u - 1))
                    col = (2 * e + w) * F + f * P
                    mm(o, w13_hi[:, col:col + P], hT_hi[b][:, :], start=True, stop=False)
                    mm(o, w13_hi[:, col:col + P], hT_lo[b][:, :], start=False, stop=False)
                    t = mm(o, w13_lo[:, col:col + P], hT_hi[b][:, :], start=False, stop=True)
                t.then_inc(xu_done, 1)

            def down(i, e):
                y = (bA, bO)[e % 2]
                pe.wait_ge(g_done, level2(g_done, i, FC * (e + 1)))
                if past(i, e - 2):
                    pe.wait_ge(yw_done, level2(yw_done, i, e - 1))
                for t4 in range(4):
                    for f in range(FC):
                        t = mm(y[:, P * t4:P * t4 + P], G[(FC * e + f) % 4][:, P * t4:P * t4 + P],
                               w2_f[:, (e % E * FC + f) * P:(e % E * FC + f + 1) * P], start=(f == 0), stop=(f == FC - 1))
                t.then_inc(y2_done, 1)

            def experts(i, b, more):
                first = isinstance(i, int) and i == 0
                for u in range(n_units):
                    unit(i, b, u)
                    e = u // FC - 1
                    if u % FC == FC - 1 and (e >= 0 or not first):
                        down(i, e)
                    if more and u == 7:
                        pre(i + 1)
                    if more and u == 9:
                        router(i + 1, 1 - b)
                if not more:
                    down(i, E - 1)

            pe.wait_ge(w13_ld, 32)
            pe.wait_ge(gate_done, 2)
            pe.wait_ge(w13_split, CHUNKS)
            pre(0)
            router(0, 0)
            run_groups(pe, experts)

        @block.scalar
        def _(act):
            def cp(out_, in_, **kw):
                return nc.scalar.activation(out_, in_, ACT.Identity if kw else ACT.Copy, **kw)

            def A1(i, n):
                k = kind_of(n)
                act.wait_ge(xT_done, level(xT_done, i, n))
                if k == SELF:
                    t = cp(xTs[:, :], bA[:, 0:P])
                elif k == CROSS:
                    cp(xTs[:, :], bA[:, 0:P], scale=norm_x)
                    t = cp(cTs[:, :], bA[:, 2 * P:3 * P])
                else:
                    t = cp(xTs[:, :], bA[:, 0:P], scale=norm_1)
                t.then_inc(xT_evac, 1)

            def A3(i, n):
                k, b = kind_of(n), n % 2
                act.wait_ge(qkT_done, level(qkT_done, i, n))
                if k == CROSS:
                    if kind_of(n - 1) == CROSS:
                        act.wait_ge(kz_pool, level(kz_pool, i, n - 1, 1))
                    cp(c_hi[:, 0, :], bQ[:, 0:P])
                    cp(c_hi[:, 1, :], bA[:, 0:P])
                    for c in range(4):
                        rows = slice(SLOT * c, SLOT * c + SLOT)
                        t = cp(Khi[b][rows, c, :], bA[rows, 0:P])
                else:
                    cp(Qs[b][0:96, :], bQ[0:96, :])
                    t = cp(K1[0:96, :], bA[0:96, 0:P])
                t.then_inc(hi_done, 1)

            def k_low(i, n):
                if kind_of(n) == CROSS:
                    act.wait_ge(lo_done, level(lo_done, i, n))
                    for c in range(4):
                        rows = slice(SLOT * c, SLOT * c + SLOT)
                        t = cp(Klo[n % 2][rows, c, :], c_lo[rows, 1, :].bitcast(F32))
                    t.then_inc(klo_done, 1)

            def A5(i, n):
                act.wait_ge(mT_done, level(mT_done, i, n))
                if kind_of(n) == CROSS:
                    for c in range(4):
                        t = cp(Qhm[n % 2][1][0:64, c, :], bS1[0:64, 0:P], scale=same_c[0:64, c:c + 1])
                    t.then_inc(m_evac_up, 1)
                else:
                    for g in range(4):
                        t = cp(Qs[n % 2][96:128, P * g:P * g + P], bS1[SLOT * g:SLOT * g + SLOT, 0:P])
                    t.then_inc(m_evac, 1)

            def B1(i, n, cs):
                for c in cs:
                    act.wait_ge(st_done, level(st_done, i, n, c + 1))
                    nc.scalar.activation(PT[c][:, :], bT[c % 2][:, :], ACT.Exp, scale=SCALE).then_inc(exp_done, 1)

            def B2(i, n):
                act.wait_ge(pv_done, level(pv_done, i, n))
                cp(OTs[:, :], bO[:, :]).then_inc(ot_evac, 1)

            def C2(i, n):
                act.wait_ge(oT_done, level(oT_done, i, n))
                kw = dict(scale=ln_g, bias=ln_b) if kind_of(n) == SELF else {}
                cp(OnT[:, :], bC[:, 0:P], **kw).then_inc(oT_evac, 1)

            def slot(i, n):
                if exists(i, n - 5):
                    C2(i, n - 5)
                if exists(i, n - 3):
                    B1(i, n - 3, [3])
                if exists(i, n - 1):
                    A3(i, n - 1)
                if exists(i, n - 2):
                    A5(i, n - 2)
                if exists(i, n - 1):
                    k_low(i, n - 1)
                if exists(i, n):
                    A1(i, n)
                if exists(i, n - 3):
                    B2(i, n - 3)
                if exists(i, n - 2):
                    B1(i, n - 2, [0, 1, 2])

            def split_w13(c):
                col = slice(CHUNK * c, CHUNK * c + CHUNK)
                act.wait_ge(w13_ld, 32)
                cp(w13_hi[:, col], w13_f[:, col]).then_inc(w13_high, 1)

            def once(n):
                if n == 1:
                    act.wait_ge(w_more, W_MORE)
                    act.wait_ge(init_pool, INIT_CROSS)
                c = n - (STEPS - 2 * CHUNKS)
                if 0 <= c < CHUNKS:
                    split_w13(c)

            run_slots(act, slot, once)

            def pre(i, b):
                act.wait_ge(pre_t, level2(pre_t, i, 1))
                cp(hT_hi[b][:, :], bQ[:, :], scale=norm_2).then_inc(pre_hi, 1)

            def route(i):
                act.wait_ge(rt, level2(rt, i, 10))
                nc.scalar.activation(ex[:, :, :], lg2[:, :, :], ACT.Exp).then_inc(rt_exp, 1)

            def experts(i, b, more):
                for u in range(n_units):
                    act.wait_ge(xu_done, level2(xu_done, i, u + 1))
                    if past(i, u - 2):
                        act.wait_ge(sg_done, level2(sg_done, i, u - 1))
                    nc.scalar.activation(th[u % 2][:, :], bS[u % 2][:, :], ACT.Tanh, scale=0.5).then_inc(tanh_done, 1)
                    if more and u == 7:
                        pre(i + 1, 1 - b)
                    if more and u == 11:
                        route(i + 1)

            pre(0, 0)
            route(0)
            run_groups(act, experts)

        @block.vector
        def _(dve):
            V = nc.vector

            def A2(i, n):
                k, b = kind_of(n), n % 2
                dve.wait_ge(qkv_done, level(qkv_done, i, n))
                if k == SELF:
                    V.tensor_tensor(T3[:, :, :, :], thrice(bA[:, P:P + 160]), thrice(b_self[:, 0:160]), ALU.add)
                    t = V.tensor_tensor(VG[n % 3][:, :, 0:HD], v3(bA[:, P + 160:P + 192], HD), v3(b_self[:, 160:192], HD), ALU.add)
                    t.then_inc(tok, 1)
                elif k == CROSS:
                    V.tensor_tensor(T[:, :], bA[:, P:3 * P], b_cross[:, 0:2 * P], ALU.add)
                    t = V.tensor_tensor(VC[n % 3][:, :, 0:HD], v3(bA[:, 3 * P:4 * P], HD), v3(b_cross[:, 2 * P:3 * P], HD), ALU.add)
                    t.then_inc(tok, 1)
                else:
                    src = v3(bA[:, P:P + 160], HD)
                    h = HD // 2
                    V.tensor_tensor(rope1[:, :, :], src, rep(cos_t, 20), ALU.mult).then_inc(tok, 1)
                    V.tensor_tensor(rope2[:, :, 0:h], src[:, :, h:HD], rep(sin_t[:, 0:h], 20), ALU.mult).then_inc(tok, 1)
                    t = V.tensor_tensor(rope2[:, :, h:HD], src[:, :, 0:h], rep(sin_t[:, h:HD], 20), ALU.mult)
                    t.then_inc(tok, 1)

            def A2b(i, n):
                if kind_of(n) == ROPE:
                    V.tensor_copy(VG[n % 3][:, :, 0:HD], v3(bA[:, P + 160:P + 192], HD))
                    dve.wait_ge(tok, level(tok, i, n, 3))
                    V.tensor_tensor(T3[:, :, :, :], thrice(rope1[:, :, :].rearrange("p a b -> p (a b)")),
                                        thrice(rope2[:, :, :].rearrange("p a b -> p (a b)")), ALU.add).then_inc(tok, 1)

            def A3(i, n):
                k, b = kind_of(n), n % 2
                dve.wait_ge(hi_done, level(hi_done, i, n))
                if k == CROSS:
                    if kind_of(n - 1) == CROSS:
                        dve.wait_ge(kz_pool, level(kz_pool, i, n - 1))
                        dve.wait_ge(klo_done, level(klo_done, i, n - 1))
                    V.tensor_tensor(c_lo[:, 0, :], bQ[:, 0:P], c_hi[:, 0, :].bitcast(F32), ALU.subtract)
                    t = V.tensor_tensor(c_lo[:, 1, :], bA[:, 0:P], c_hi[:, 1, :].bitcast(F32), ALU.subtract)
                    t.then_inc(lo_done, 1)
                else:
                    V.tensor_tensor(Qs[b][32:64, :], bQ[32:64, :], Qs[b][32:64, :].bitcast(F32), ALU.subtract)
                    t = V.tensor_tensor(K1[64:96, :], bA[64:96, 0:P], K1[64:96, :].bitcast(F32), ALU.subtract)
                    t.then_inc(lo_done, 1)

            def mask_heads(i, n):
                k, b = kind_of(n), n % 2
                if k == CROSS:
                    t = V.tensor_tensor(Qhm[b][0][:, :, :], rep(c_hi[:, 0, :].bitcast(F32), 4), last(same_c, P), ALU.mult)
                    t.then_inc(kz_done, 1)
                else:
                    dve.wait_ge(lo_done, level(lo_done, i, n))
                    t = V.tensor_tensor(Kz[b][0:96, :, :], rep(K1[0:96, :].bitcast(F32), 4), last(same_c[0:96, :], P), ALU.mult)
                    t.then_inc(kz_done, 1)

            def A4(i, n, gs):
                k = kind_of(n)
                for g in gs:
                    dve.wait_ge(s_done, level(s_done, i, n, g + 1))
                    dst = negmax[:, g, :] if k != CROSS else negmax[:, :, g]
                    V.tensor_reduce(dst, v3(bS[g % 2][:, :], P), AX.X, ALU.max, negate=True).then_inc(s_max, 1)

            def max_parts(n):
                if kind_of(n) == CROSS:
                    return negmax[:, :, :].rearrange("p a b -> p (a b)"), MxC[:, :, 0], MxC[:, :, 1]
                mv = MxG[:, :, :].rearrange("p g (c d) -> p g c d", d=HD)
                return negmax[:, :, :], mv[:, :, :, 0], mv[:, :, :, 1]

            def M1(i, n):
                flat, hi, lo = max_parts(n)
                dve.wait_ge(s_max, level(s_max, i, n))
                V.tensor_copy(hi.bitcast(F32R), flat).then_inc(m_hi, 1)

            def M2(i, n):
                flat, hi, lo = max_parts(n)
                dve.wait_ge(m_hi, level(m_hi, i, n))
                V.tensor_tensor(lo, flat, hi, ALU.subtract).then_inc(m_done, 1)

            def A5(i, n):
                if kind_of(n) == CROSS:
                    dve.wait_ge(mT_done, level(mT_done, i, n))
                    V.tensor_tensor(Qhm[n % 2][0][64:128, :, :], rep(bS1[64:128, 0:P], 4), last(same_c[64:128, :], P),
                                    ALU.mult).then_inc(m_evac, 1)

            def C1(i, n):
                k = kind_of(n)
                dve.wait_ge(on_done, level(on_done, i, n))
                ov = bC[:, :].rearrange("p (g c d) -> p g c d", c=4, d=SLOT)
                V.reciprocal(rec[:, :, :], ov[:, :, :, HD]).then_inc(c_dve, 1)
                dve.wait_ge(c_dve, level(c_dve, i, n, 1))
                dst = On[:, :].rearrange("p (g c d) -> p g c d", c=4, d=HD)
                r4 = rec[:, :, :].unsqueeze(3).to_broadcast([P, 4, 4, HD])
                t = V.tensor_tensor(dst, ov[:, :, :, 0:HD], r4, ALU.mult)
                if k != SELF:
                    t.then_inc(o_ready, 1)
                    return
                t.then_inc(c_dve, 1)
                dve.wait_ge(c_dve, level(c_dve, i, n, 2))
                V.bn_stats(st_in[:, :], On[:, :]).then_inc(c_dve, 1)
                dve.wait_ge(c_dve, level(c_dve, i, n, 3))
                dve.sem_inc(waits_carried, 1)
                V.bn_aggr(mv_in[:, :], st_in[:, :]).then_inc(c_dve, 1)

            def C1b(i, n):
                if kind_of(n) == SELF:
                    dve.wait_ge(ln_in, level(ln_in, i, n))
                    V.tensor_scalar(On2[:, :], On[:, :], mv_in[:, 0:1], rs_in[:, 1:2], ALU.subtract, ALU.mult).then_inc(o_ready, 1)

            def C3(i, n):
                k, j = kind_of(n), n % STREAMS
                dve.wait_ge(y_done, level(y_done, i, n))
                if k == ROPE:
                    t = V.tensor_tensor(X3[:, bass.ds(((i + n // STEPS) * STREAMS + j) * P, P)], bC[:, P:2 * P], XS[j][:, :], ALU.add)
                    t.then_inc(res, 1)
                    return
                dve.wait_ge(xb_done, level(xb_done, i, n))
                if exists(i, n - 1) and kind_of(n - 1) != ROPE:
                    dve.wait_ge(xs_done, level(xs_done, i, n - 1))
                V.tensor_tensor(R[:, :], bC[:, P:2 * P], XB[j][:, :], ALU.add).then_inc(res, 1)

            def C4(i, n):
                if kind_of(n) != ROPE:
                    dve.wait_ge(res, level(res, i, n))
                    V.bn_stats(st_post[:, :], R[:, :]).then_inc(post, 1)

            def C5(i, n):
                if kind_of(n) != ROPE:
                    dve.wait_ge(post, level(post, i, n, 1))
                    dve.sem_inc(waits_carried, 1)
                    V.bn_aggr(mv_post[:, :], st_post[:, :]).then_inc(post, 1)

            def D(i, n):
                k, j = kind_of(n), n % STREAMS
                if k == ROPE:
                    return
                dve.wait_ge(ln_post, level(ln_post, i, n))
                V.tensor_scalar(H[j][:, :], R[:, :], mv_post[:, 0:1], rs_post[:, 4:5], ALU.subtract, ALU.mult).then_inc(h_done, 1)
                V.tensor_scalar(XS[j][:, :], R[:, :], mv_post[:, 0:1], rs_post[:, 3:4], ALU.subtract, ALU.mult).then_inc(xs_done, 1)

            def slot(i, n):
                if exists(i, n - 5):
                    C4(i, n - 5)
                if exists(i, n - 2):
                    M2(i, n - 2)
                if exists(i, n - 1):
                    A3(i, n - 1)
                if exists(i, n - 2):
                    A5(i, n - 2)
                if exists(i, n - 1):
                    mask_heads(i, n - 1)
                if exists(i, n - 5):
                    C5(i, n - 5)
                if exists(i, n - 4):
                    C1(i, n - 4)
                if exists(i, n - 1):
                    A4(i, n - 1, [0, 1])
                if exists(i, n - 4):
                    C1b(i, n - 4)
                if exists(i, n):
                    A2(i, n)
                    A2b(i, n)
                if exists(i, n - 5):
                    D(i, n - 5)
                if exists(i, n - 1):
                    A4(i, n - 1, [2, 3])
                if exists(i, n - 4):
                    C3(i, n - 4)
                if exists(i, n - 1):
                    M1(i, n - 1)

            dve.wait_ge(w_ld, W_FIRST)
            V.tensor_copy(ident_b[:, :], ident[:, :])
            V.tensor_copy(mask_b[:, :, :], rep(mask_f[:, :], 4)).then_inc(init_dve, 1)
            dve.wait_ge(init_pool, INIT_V)
            run_slots(dve, slot)

            dve.wait_ge(w_more, W_MORE)
            V.tensor_copy(gate_r[:, 0, :], gate_f[:, :]).then_inc(gate_done, 1)
            dve.wait_ge(gate_done, 1)
            V.tensor_tensor(gate_r[:, 1, :], gate_f[:, :], gate_r[:, 0, :].bitcast(F32), ALU.subtract).then_inc(gate_done, 1)

            def x3(i, t4):
                return X3[:, bass.ds((i * GROUP + t4) * P, P)]

            def pre(i, b):
                for t4 in range(4):
                    V.bn_stats(st4[:, t4, :], x3(i, t4)).then_inc(pre_st, 1)
                for t4 in range(4):
                    dve.wait_ge(pre_st, level2(pre_st, i, t4 + 1))
                    dve.sem_inc(waits_carried, 1)
                    t = V.bn_aggr(mv4[:, t4, :], st4[:, t4, :])
                t.then_inc(pre_st, 1)
                dve.wait_ge(pre_st, level2(pre_st, i, 5))
                V.tensor_tensor(q4[:, :, 0:1], mv4[:, :, 0:1], mv4[:, :, 0:1], ALU.mult).then_inc(pre_q, 1)

            def pre1(i, b):
                dve.wait_ge(pre_rs, level2(pre_rs, i, 1))
                for t4 in range(4):
                    V.tensor_scalar(H2[:, t4, :], x3(i, t4), rs4[:, t4, :], None, ALU.mult).then_inc(pre_h, 1)

            def pre2(i, b):
                dve.wait_ge(pre_hi, level2(pre_hi, i, 1))
                V.scalar_tensor_tensor(hT_lo[b][:, :], bQ[:, :], norm_2, hT_hi[b][:, :].bitcast(F32), ALU.mult,
                                       ALU.subtract).then_inc(pre_lo, 1)

            def route1(i):
                dve.wait_ge(pre_g, level2(pre_g, i, 1))
                V.tensor_copy(lg[:, :, :], v3(bC[:, 0:4 * E], E)).then_inc(rt, 1)
                dve.wait_ge(rt, level2(rt, i, 1))
                dve.sem_inc(waits_carried, 1)
                for t4 in range(4):
                    V.max(top8[:, t4, :], lg[:, t4, :]).then_inc(rt, 1)

            def route1b(i):
                for t4 in range(4):
                    dve.wait_ge(rt, level2(rt, i, 2 + t4))
                    dve.sem_inc(waits_carried, 1)
                    V.max_index(idx8[:, t4, :], top8[:, t4, :], lg[:, t4, :]).then_inc(rt, 1)
                V.tensor_tensor(lg2[:, :, :], lg[:, :, :], top8[:, :, 0:1].to_broadcast([P, 4, E]), ALU.subtract
                                ).then_inc(rt, 1)

            def route2(i, b):
                dve.wait_ge(rt, level2(rt, i, 9))
                V.tensor_copy(idxf[:, :, :], idx8[:, :, :]).then_inc(rt, 1)
                dve.wait_ge(rt, level2(rt, i, 11))
                io = rep(iota_e, 4)
                V.tensor_tensor(hot[:, :, :], io, idxf[:, :, 0:1].to_broadcast([P, 4, E]), ALU.is_equal).then_inc(rt, 1)
                V.tensor_tensor(hot2[:, :, :], io, idxf[:, :, 1:2].to_broadcast([P, 4, E]), ALU.is_equal).then_inc(rt, 1)
                dve.wait_ge(rt, level2(rt, i, 13))
                V.tensor_tensor(hot[:, :, :], hot[:, :, :], hot2[:, :, :], ALU.add).then_inc(rt, 1)

            def route2b(i, b):
                dve.wait_ge(rt_exp, level2(rt_exp, i, 1))
                dve.wait_ge(rt, level2(rt, i, 14))
                V.tensor_tensor(hot2[:, :, :], hot[:, :, :], ex[:, :, :], ALU.mult).then_inc(rt, 1)
                dve.wait_ge(rt, level2(rt, i, 15))
                V.tensor_reduce(wsum[:, :, 0], hot2[:, :, :], AX.X, ALU.add).then_inc(rt, 1)
                dve.wait_ge(rt, level2(rt, i, 16))
                V.reciprocal(wrec[:, :, :], wsum[:, :, :]).then_inc(rt, 1)
                dve.wait_ge(rt, level2(rt, i, 17))
                V.scalar_tensor_tensor(Wr[b][:, :, :], hot2[:, :, :], 0.5, wrec[:, :, :].to_broadcast([P, 4, E]),
                                       ALU.mult, ALU.mult).then_inc(wr_done, 1)

            def weigh(i, b, e):
                dve.wait_ge(y2_done, level2(y2_done, i, e + 1))
                if past(i, e - 2):
                    dve.wait_ge(acc_done, level2(acc_done, i, e - 1))
                y = (bA, bO)[e % 2]
                V.tensor_tensor(yw[e % 2][:, :, :], v3(y[:, :], P), Wr[b][:, :, e % E:e % E + 1].to_broadcast([P, 4, P]),
                                ALU.mult).then_inc(yw_done, 1)

            def final1(i, b):
                dve.wait_ge(acc_done, level2(acc_done, i, E))
                for t4 in range(4):
                    V.bn_stats(st_f[:, t4, :], acc[b][:, t4, :]).then_inc(fin_st, 1)
                for t4 in range(4):
                    dve.wait_ge(fin_st, level2(fin_st, i, t4 + 1))
                    dve.sem_inc(waits_carried, 1)
                    t = V.bn_aggr(mv_f[:, t4, :], st_f[:, t4, :])
                t.then_inc(fin_st, 1)

            def final2(i, b):
                dve.wait_ge(fin_rs, level2(fin_rs, i, 2))
                if not (isinstance(i, int) and i < 2):
                    dve.wait_ge(out_done[b], 8 * (i - b))
                for t4 in range(4):
                    V.tensor_scalar(fin[b][:, t4, :], acc[b][:, t4, :], mv_f[:, t4, 0:1], rs_f[:, t4, 1:2], ALU.subtract,
                                    ALU.mult).then_inc(fin_done, 1)

            def experts(i, b, more):
                first = isinstance(i, int) and i == 0
                for u in range(n_units):
                    dve.wait_ge(tanh_done, level2(tanh_done, i, u + 1))
                    V.scalar_tensor_tensor(sg[u % 2][:, :], th[u % 2][:, :], 1.0, bS[u % 2][:, :], ALU.add, ALU.mult
                                           ).then_inc(sg_done, 1)
                    dve.wait_ge(sg_done, level2(sg_done, i, u + 1))
                    if past(i, u - 4):
                        dve.wait_ge(y2_done, level2(y2_done, i, (u - 4) // FC + 1))
                    V.tensor_tensor(G[u % 4][:, :], sg[u % 2][:, :], bT[u % 2][:, :], ALU.mult).then_inc(g_done, 1)
                    e = u // FC - 2
                    if u % FC == 0 and (e >= 0 or not first):
                        weigh(i, b if e >= 0 else 1 - b, e)
                    if more:
                        if u == 3:
                            pre(i + 1, 1 - b)
                        if u == 5:
                            pre1(i + 1, 1 - b)
                        if u == 8:
                            pre2(i + 1, 1 - b)
                        if u == 10:
                            route1(i + 1)
                        if u == 11:
                            route1b(i + 1)
                        if u == 13:
                            route2(i + 1, 1 - b)
                        if u == 14:
                            route2b(i + 1, 1 - b)
                    if not first and u == 6:
                        final1(i - 1, 1 - b)
                    if not first and u == 9:
                        final2(i - 1, 1 - b)
                if not more:
                    weigh(i, b, E - 2)
                    weigh(i, b, E - 1)

            pre(0, 0)
            pre1(0, 0)
            pre2(0, 0)
            route1(0)
            route1b(0)
            route2(0, 0)
            route2b(0, 0)
            run_groups(dve, experts)
            final1(GROUPS - 1, 1)
            final2(GROUPS - 1, 1)

        @block.gpsimd
        def _(pool):
            G_ = nc.gpsimd

            def xb(i, n):
                k, j = kind_of(n), n % STREAMS
                if k == ROPE:
                    return
                if k == SELF:
                    pool.wait_ge(x_ld[j], 16 * (i + 1))
                    if exists(i, n - STREAMS):
                        pool.wait_ge(res, level(res, i, n - STREAMS))
                else:
                    pool.wait_ge(xs_done, level(xs_done, i, n - STREAMS))
                src = XL[j] if k == SELF else XS[j]
                G_.tensor_tensor(XB[j][:, :], src[:, :], b_out[k], ALU.add).then_inc(xb_done, 1)

            def q_upper(i, n):
                if kind_of(n) == CROSS:
                    pool.wait_ge(hi_done, level(hi_done, i, n))
                    G_.tensor_tensor(Qhm[n % 2][1][:, :, :], rep(c_hi[:, 0, :].bitcast(F32), 4), last(same_c, P), ALU.mult
                                     ).then_inc(kz_pool, 1)

            def q_low(i, n):
                if kind_of(n) == CROSS:
                    pool.wait_ge(lo_done, level(lo_done, i, n))
                    G_.tensor_tensor(Qlo[n % 2][:, :, :], rep(c_lo[:, 0, :].bitcast(F32), 4), last(same_c, P), ALU.mult
                                     ).then_inc(kz_pool, 1)

            def sel(i, n, cs):
                if kind_of(n) == CROSS:
                    return
                for c in cs:
                    pool.wait_ge(exp_done, level(exp_done, i, n, c + 1))
                    pool.sem_inc(waits_carried, 1)
                    G_.affine_select(out=v3(PT[c][:, :], P), in_=v3(PT[c][:, :], P), pattern=[[0, 4], [1, P]],
                                         compare_op=ALU.is_ge, fill=0.0, base=0, channel_multiplier=-1).then_inc(causal, 1)

            def rs_inner(i, n):
                if kind_of(n) != SELF:
                    return
                pool.wait_ge(c_dve, level(c_dve, i, n))
                G_.tensor_tensor(rs_in[:, 0:1], mv_in[:, 1:2], eps_col, ALU.add).then_inc(ln_in, 1)
                pool.wait_ge(ln_in, level(ln_in, i, n, 1))
                G_.tensor_tensor(rs_in[:, 1:2], rs_in[:, 0:1], minus_half, ALU.pow).then_inc(ln_in, 1)

            def rs_after(i, n):
                if kind_of(n) == ROPE:
                    pool.wait_ge(res, level(res, i, n))
                    col = bass.ds(((i + n // STEPS) * STREAMS + n % STREAMS) * P, P)
                    G_.tensor_tensor(X23[:, col], X3[:, col], XS[n % STREAMS][:, :], ALU.add).then_inc(x23_done, 1)
                    return
                pool.wait_ge(post, level(post, i, n))
                G_.tensor_tensor(rs_post[:, 0:1], mv_post[:, 1:2], eps_col, ALU.add).then_inc(ln_post, 1)
                pool.wait_ge(ln_post, level(ln_post, i, n, 1))
                G_.tensor_tensor(rs_post[:, 2:3], rs_post[:, 0:1], eps_col, ALU.mult).then_inc(ln_post, 1)
                pool.wait_ge(ln_post, level(ln_post, i, n, 2))
                G_.tensor_tensor(rs_post[:, 1:2], rs_post[:, 2:3], mv_post[:, 1:2], ALU.add).then_inc(ln_post, 1)
                pool.wait_ge(ln_post, level(ln_post, i, n, 3))
                G_.tensor_tensor(rs_post[:, 3:5], rs_post[:, 0:2], minus_half.to_broadcast([P, 2]), ALU.pow).then_inc(ln_post, 1)

            def slot(i, n):
                if exists(i, n):
                    xb(i, n)
                if exists(i, n - 2):
                    q_upper(i, n - 2)
                if exists(i, n - 6):
                    rs_after(i, n - 6)
                if exists(i, n - 5):
                    rs_inner(i, n - 5)
                if exists(i, n - 3):
                    sel(i, n - 3, [0, 1, 2])
                if exists(i, n - 2):
                    q_low(i, n - 2)
                if exists(i, n - 3):
                    sel(i, n - 3, [3])

            def split_w13(c):
                col = slice(CHUNK * c, CHUNK * c + CHUNK)
                pool.wait_ge(w13_high, c + 1)
                G_.tensor_tensor(w13_lo[:, col], w13_f[:, col], w13_hi[:, col].bitcast(F32), ALU.subtract).then_inc(w13_split, 1)

            G_.memset(MxG[:, :, :], 0.0)
            G_.memset(MxC[:, :, :], 0.0)
            G_.memset(ones_f[:, :], 1.0)
            for b in range(3):
                G_.memset(VG[b][:, :, :], 0.0)
                G_.memset(VC[b][:, :, :], 0.0)
            pool_set = G_.memset(rs_in[:, :], 0.0)
            pool_set.then_inc(pool_zero, 1)
            pool.wait_ge(pool_zero, 1)
            for b in range(3):
                G_.memset(VG[b][:, :, HD:HD + 1], 1.0)
                t = G_.memset(VC[b][:, :, HD:HD + 1], 1.0)
            t.then_inc(init_pool, 1)
            pool.wait_ge(w_ld, W_FIRST)
            pool.wait_ge(init_pool, INIT_V)
            for b in range(2):
                t = G_.tensor_tensor(Kz[b][96:128, :, :], rep(ones_f[96:128, :], 4), last(slot3_one[96:128, :], P), ALU.mult)
            t.then_inc(init_pool, 1)
            pool.wait_ge(init_pool, INIT_KZ)
            for b in range(2):
                G_.tensor_tensor(Khi[b][:, :, :], rep(ones_f[:, :], 4), rep(ones_f[:, :], 4), ALU.subtract)
                t = G_.tensor_tensor(Klo[b][:, :, :], rep(ones_f[:, :], 4), last(max_one, P), ALU.mult)
            t.then_inc(init_pool, 1)
            def once(n):
                if n >= STEPS - CHUNKS:
                    split_w13(n - (STEPS - CHUNKS))

            run_slots(pool, slot, once)

            def pre(i):
                pool.wait_ge(pre_q, level2(pre_q, i, 1))
                G_.tensor_tensor(q4[:, :, 1:2], q4[:, :, 0:1], mv4[:, :, 1:2], ALU.add).then_inc(pre_pool, 1)
                pool.wait_ge(pre_pool, level2(pre_pool, i, 1))
                G_.tensor_tensor(q4[:, :, 0:1], q4[:, :, 1:2], rep(eps_col, 4), ALU.add).then_inc(pre_pool, 1)
                pool.wait_ge(pre_pool, level2(pre_pool, i, 2))
                G_.tensor_tensor(rs4[:, :, :], q4[:, :, 0:1], rep(minus_half, 4), ALU.pow).then_inc(pre_rs, 1)

            def accumulate(i, b, e):
                pool.wait_ge(yw_done, level2(yw_done, i, e + 1))
                if e == 0:
                    if not (isinstance(i, int) and i < 2):
                        pool.wait_ge(fin_done, level2(fin_done, i - 2, 4))
                    src = v3(X23[:, bass.ds(i * N, N)], P)
                else:
                    pool.wait_ge(acc_done, level2(acc_done, i, e))
                    src = acc[b][:, :, :]
                G_.tensor_tensor(acc[b][:, :, :], src, yw[e % 2][:, :, :], ALU.add).then_inc(acc_done, 1)

            def final(i):
                pool.wait_ge(fin_st, level2(fin_st, i, 5))
                G_.tensor_tensor(rs_f[:, :, 0:1], mv_f[:, :, 1:2], rep(eps_col, 4), ALU.add).then_inc(fin_rs, 1)
                pool.wait_ge(fin_rs, level2(fin_rs, i, 1))
                G_.tensor_tensor(rs_f[:, :, 1:2], rs_f[:, :, 0:1], rep(minus_half, 4), ALU.pow).then_inc(fin_rs, 1)

            def experts(i, b, more):
                first = isinstance(i, int) and i == 0
                if not first:
                    accumulate(i, 1 - b, -2)
                    accumulate(i, 1 - b, -1)
                if more:
                    pre(i + 1)
                if not first:
                    final(i - 1)
                for e in range(E if not more else E - 2):
                    accumulate(i, b, e)

            pre(0)
            pool.wait_ge(x23_done, level(x23_done, ITER, -1))
            run_groups(pool, experts)
            final(GROUPS - 1)



def kernel(**inputs):
    import numpy as np
    import concourse.bacc as bacc
    from concourse.bass_utils import run_bass_kernel_spmd as run

    a = {k: np.asarray(v) for k, v in inputs.items()}
    C = np.ascontiguousarray
    f = np.float32
    T = 128

    def q_order(w):
        return w.reshape(4, 4, 8, -1).transpose(1, 0, 2, 3).reshape(128, -1)

    wqkv = a["L0_ffn_wqkv"]
    w_rope = np.concatenate([q_order(wqkv[:128]), wqkv[128:]], axis=0).T
    wo_rope = q_order(a["L0_ffn_wo"].T)
    rows = np.concatenate([a[k] for k in ("L0_attn_bq", "L0_attn_bk", "L0_attn_bv", "L0_xattn_b_q", "L0_xattn_b_kv",
                                          "L0_attn_bo", "L0_xattn_b_out")])
    feat = np.stack([a[k] for k in ("L0_attn_ln_g", "L0_attn_ln_b", "L0_xattn_w_norm", "L0_ffn_ln1_w", "L0_ffn_ln2_w")], axis=1)

    p = np.arange(128)
    k4 = np.arange(4)
    same_c = ((p % 32) // 8)[:, None] == k4
    max_block = (p // 32)[:, None] == (k4 + 2) % 4
    inv_freq = f(1.0) / (f(10000.0) ** (np.arange(0, 8, 2, dtype=f) / f(8)))
    ang = np.arange(T, dtype=f)[:, None] * inv_freq[None, :]
    cos, sin = np.cos(ang), np.sin(ang)
    two = (p % 8 < 2)[:, None]
    tables = np.concatenate([same_c, max_block, cos, cos, -sin, sin, same_c & two, max_block & two,
                             np.tile(np.arange(8), (128, 1)), np.full((128, 1), -0.5), np.full((128, 1), EPS)], axis=1).astype(f)
    mask = np.where(p[None, :] > p[:, None], f(NEG), f(0)).astype(f)

    E = a["L0_ffn_gate_w"].shape[0]
    arrays = {
        "x": a["x"],
        "ctx_in": a["ctx_1024"],
        "w_self": np.concatenate([a["L0_attn_Wq"], a["L0_attn_Wk"], a["L0_attn_Wv"]], axis=1),
        "w_crossq": a["L0_xattn_w_q"].T,
        "w_crosskv": a["L0_xattn_w_kv"].T,
        "w_rope": w_rope,
        "w_out": np.stack([a["L0_attn_Wo"], a["L0_xattn_w_out"].T, wo_rope]),
        "bias_rows": np.broadcast_to(rows, (128, rows.size)),
        "feat_cols": feat,
        "tables": tables,
        "ident_in": np.eye(128, dtype=f),
        "mask_in": mask,
        "gate_in": a["L0_ffn_gate_w"].T,
        "w13_in": a["L0_ffn_w13"].transpose(2, 0, 1).reshape(128, -1),
        "w2_in": a["L0_ffn_w2"].reshape(E, 128, -1, 128).transpose(3, 0, 2, 1).reshape(128, -1),
    }
    nc = bacc.Bacc("TRN2", target_bir_lowering=False, num_devices=1)
    arrays = {k: C(v) for k, v in arrays.items()}
    aps = [nc.dram_tensor(k, v.shape, mybir.dt.from_np(v.dtype), kind="ExternalInput").ap() for k, v in arrays.items()]
    out = nc.dram_tensor("out", a["x"].shape, F32, kind="ExternalOutput").ap()
    program(nc, *aps, out)
    r = run(nc, [arrays], core_ids=[0])
    return r.results[0]["out"]
```
